# Optimizing a Trainium2 kernel written in Bass

```python
import numpy as np
import jax
import jax.numpy as jnp

def _softmax(x, axis=-1):
    return jax.nn.softmax(x, axis=axis)

def _gelu(x):
    return jax.nn.gelu(x, approximate=True)

def _silu(x):
    return jax.nn.silu(x)

def _sigmoid(x):
    return jax.nn.sigmoid(x)

def _layernorm(x, axis=-1, eps=1e-05):
    m = jnp.mean(x, axis=axis, keepdims=True)
    v = jnp.var(x, axis=axis, keepdims=True)
    return (x - m) / jnp.sqrt(v + eps)

def _scatter_add(tgt, idx, src, axis=0):
    return tgt.at[idx].add(src)

def _segment_sum(src, seg, n):
    return jax.ops.segment_sum(src, seg, n)
kernel_name = 'mk_conv_seq_d4_conv_nchw512_r4_082464'

def setup_inputs(seed: int=0):
    np.random.seed(seed)
    _w = jnp.asarray

    def _rec_inputs():
        import jax
        import jax.numpy as jnp
        _gk = jax.random.key(seed)
        x = -0.0002928 + 1 * jax.random.normal(jax.random.fold_in(_gk, 1), (2, 128, 16, 16), jnp.float32)
        return x
    x = _rec_inputs()

    def _L0_conv_setup():
        import jax, jax.numpy as jnp
        import numpy as np
        C = 128
        HEADS = 8
        DH = 16
        G = 32
        EPS = 1e-05
        SCALE = DH ** (-0.25)
        key = jax.random.key(seed)
        ks = jax.random.split(key, 10)
        B, H, W = (2, 16, 16)

        def w(k):
            return jax.random.normal(k, (C, C), jnp.float32) * 0.02

        def b(k):
            return jax.random.normal(k, (C,), jnp.float32) * 0.02
        return {'x': jax.random.normal(ks[0], (B, C, H, W), jnp.float32), 'gn_w': jnp.ones((C,), jnp.float32), 'gn_b': jnp.zeros((C,), jnp.float32), 'wq': w(ks[1]), 'bq': b(ks[2]), 'wk': w(ks[3]), 'bk': b(ks[4]), 'wv': w(ks[5]), 'bv': b(ks[6]), 'wp': w(ks[7]), 'bp': b(ks[8])}
    _L0_conv_all = _L0_conv_setup()
    _L0_conv_in = {k: v for k, v in _L0_conv_all.items() if k in ('gn_w', 'gn_b', 'wq', 'bq', 'wk', 'bk', 'wv', 'bv', 'wp', 'bp')}
    del _L0_conv_all

    def _L1_conv_setup():
        import jax, jax.numpy as jnp
        import numpy as np
        C = 128
        GROUPS = 32
        HEAD_CH = 16
        HEADS = C // HEAD_CH
        EPS = 1e-05
        key = jax.random.key(seed)
        ks = jax.random.split(key, 7)
        orig_batch = jax.random.normal(ks[0], (16, C, 32, 32), dtype=jnp.float32)
        gn_w = jax.random.normal(ks[1], (C,), dtype=jnp.float32) * 0.02 + 1.0
        gn_b = jax.random.normal(ks[2], (C,), dtype=jnp.float32) * 0.02
        w1 = jax.random.normal(ks[3], (3 * C, C), dtype=jnp.float32) * (1.0 / np.sqrt(C))
        b1 = jax.random.normal(ks[4], (3 * C,), dtype=jnp.float32) * 0.01
        w2 = jax.random.normal(ks[5], (C, C), dtype=jnp.float32) * (1.0 / np.sqrt(C))
        b2 = jax.random.normal(ks[6], (C,), dtype=jnp.float32) * 0.01
        return {'orig_batch': orig_batch, 'gn_w': gn_w, 'gn_b': gn_b, 'w1': w1, 'b1': b1, 'w2': w2, 'b2': b2}
    _L1_conv_all = _L1_conv_setup()
    _L1_conv_in = {k: v for k, v in _L1_conv_all.items() if k in ('gn_w', 'gn_b', 'w1', 'b1', 'w2', 'b2')}
    del _L1_conv_all

    def _L2_conv_setup():
        import jax, jax.numpy as jnp
        import numpy as np
        import math
        NUM_GROUPS = 32
        NUM_HEADS = 8
        EPS = 1e-05

        def _group_norm(x, weight, bias):
            b, c, h, w = x.shape
            xg = x.reshape(b, NUM_GROUPS, c // NUM_GROUPS, h, w)
            mean = jnp.mean(xg, axis=(2, 3, 4), keepdims=True)
            var = jnp.var(xg, axis=(2, 3, 4), keepdims=True)
            xn = ((xg - mean) * jax.lax.rsqrt(var + EPS)).reshape(b, c, h, w)
            return xn * weight[None, :, None, None] + bias[None, :, None, None]
        key = jax.random.key(seed)
        ks = jax.random.split(key, 4)
        b, c, h, w = (2, 128, 16, 16)
        s = 1.0 / math.sqrt(c)
        return {'x': jax.random.normal(ks[0], (b, c, h, w), dtype=jnp.float32), 'gn_weight': jnp.ones((c,), jnp.float32), 'gn_bias': jnp.zeros((c,), jnp.float32), 'wq': jax.random.normal(ks[1], (c, c), jnp.float32) * s, 'bq': jnp.zeros((c,), jnp.float32), 'wkv': jax.random.normal(ks[2], (2 * c, c), jnp.float32) * s, 'bkv': jnp.zeros((2 * c,), jnp.float32), 'wproj': jax.random.normal(ks[3], (c, c), jnp.float32) * s, 'bproj': jnp.zeros((c,), jnp.float32)}
    _L2_conv_all = _L2_conv_setup()
    _L2_conv_in = {k: v for k, v in _L2_conv_all.items() if k in ('gn_weight', 'gn_bias', 'wq', 'bq', 'wkv', 'bkv', 'wproj', 'bproj')}
    del _L2_conv_all

    def _L3_conv_setup():
        import jax, jax.numpy as jnp
        import numpy as np
        NUM_GROUPS = 32
        EPS = 1e-06

        def _group_norm(x, scale, bias):
            b, c, h, w = x.shape
            xr = x.reshape(b, NUM_GROUPS, c // NUM_GROUPS, h, w)
            mean = xr.mean(axis=(2, 3, 4), keepdims=True)
            var = xr.var(axis=(2, 3, 4), keepdims=True)
            xn = ((xr - mean) * jax.lax.rsqrt(var + EPS)).reshape(b, c, h, w)
            return xn * scale[None, :, None, None] + bias[None, :, None, None]
        key = jax.random.key(seed)
        ks = jax.random.split(key, 5)
        B, C, H, W = (4, 128, 16, 16)
        x = jax.random.normal(ks[0], (B, C, H, W), dtype=jnp.float32)
        gn_scale = jnp.ones((C,), jnp.float32)
        gn_bias = jnp.zeros((C,), jnp.float32)
        qkv_w = jax.random.normal(ks[1], (3 * C, C), dtype=jnp.float32) * C ** (-0.5)
        qkv_b = jnp.zeros((3 * C,), jnp.float32)
        proj_w = jax.random.normal(ks[2], (C, C), dtype=jnp.float32) * C ** (-0.5)
        proj_b = jnp.zeros((C,), jnp.float32)
        return {'x': x, 'gn_scale': gn_scale, 'gn_bias': gn_bias, 'qkv_w': qkv_w, 'qkv_b': qkv_b, 'proj_w': proj_w, 'proj_b': proj_b}
    _L3_conv_all = _L3_conv_setup()
    _L3_conv_in = {k: v for k, v in _L3_conv_all.items() if k in ('gn_scale', 'gn_bias', 'qkv_w', 'qkv_b', 'proj_w', 'proj_b')}
    del _L3_conv_all
    return {'x': x, 'L0_conv_gn_w': _L0_conv_in['gn_w'], 'L0_conv_gn_b': _L0_conv_in['gn_b'], 'L0_conv_wq': _L0_conv_in['wq'], 'L0_conv_bq': _L0_conv_in['bq'], 'L0_conv_wk': _L0_conv_in['wk'], 'L0_conv_bk': _L0_conv_in['bk'], 'L0_conv_wv': _L0_conv_in['wv'], 'L0_conv_bv': _L0_conv_in['bv'], 'L0_conv_wp': _L0_conv_in['wp'], 'L0_conv_bp': _L0_conv_in['bp'], 'L1_conv_gn_w': _L1_conv_in['gn_w'], 'L1_conv_gn_b': _L1_conv_in['gn_b'], 'L1_conv_w1': _L1_conv_in['w1'], 'L1_conv_b1': _L1_conv_in['b1'], 'L1_conv_w2': _L1_conv_in['w2'], 'L1_conv_b2': _L1_conv_in['b2'], 'L2_conv_gn_weight': _L2_conv_in['gn_weight'], 'L2_conv_gn_bias': _L2_conv_in['gn_bias'], 'L2_conv_wq': _L2_conv_in['wq'], 'L2_conv_bq': _L2_conv_in['bq'], 'L2_conv_wkv': _L2_conv_in['wkv'], 'L2_conv_bkv': _L2_conv_in['bkv'], 'L2_conv_wproj': _L2_conv_in['wproj'], 'L2_conv_bproj': _L2_conv_in['bproj'], 'L3_conv_gn_scale': _L3_conv_in['gn_scale'], 'L3_conv_gn_bias': _L3_conv_in['gn_bias'], 'L3_conv_qkv_w': _L3_conv_in['qkv_w'], 'L3_conv_qkv_b': _L3_conv_in['qkv_b'], 'L3_conv_proj_w': _L3_conv_in['proj_w'], 'L3_conv_proj_b': _L3_conv_in['proj_b']}

def reference(x, L0_conv_gn_w, L0_conv_gn_b, L0_conv_wq, L0_conv_bq, L0_conv_wk, L0_conv_bk, L0_conv_wv, L0_conv_bv, L0_conv_wp, L0_conv_bp, L1_conv_gn_w, L1_conv_gn_b, L1_conv_w1, L1_conv_b1, L1_conv_w2, L1_conv_b2, L2_conv_gn_weight, L2_conv_gn_bias, L2_conv_wq, L2_conv_bq, L2_conv_wkv, L2_conv_bkv, L2_conv_wproj, L2_conv_bproj, L3_conv_gn_scale, L3_conv_gn_bias, L3_conv_qkv_w, L3_conv_qkv_b, L3_conv_proj_w, L3_conv_proj_b):
    import jax
    import jax.numpy as jnp

    def _L0_conv_ref(x, gn_w, gn_b, wq, bq, wk, bk, wv, bv, wp, bp):
        import jax, jax.numpy as jnp
        import numpy as np
        C = 128
        HEADS = 8
        DH = 16
        G = 32
        EPS = 1e-05
        SCALE = DH ** (-0.25)
        B, Cc, H, W = x.shape
        xr = x.reshape(B, G, Cc // G, H * W)
        mean = xr.mean(axis=(2, 3), keepdims=True)
        var = xr.var(axis=(2, 3), keepdims=True)
        h = ((xr - mean) * jax.lax.rsqrt(var + EPS)).reshape(B, Cc, H, W)
        h = h * gn_w[None, :, None, None] + gn_b[None, :, None, None]
        t = h.reshape(B, Cc, H * W).transpose(0, 2, 1)
        q = (t @ wq.T + bq) * SCALE
        k = (t @ wk.T + bk) * SCALE
        v = t @ wv.T + bv

        def split_heads(a):
            return a.reshape(B, H * W, HEADS, DH).transpose(0, 2, 1, 3)
        q, k, v = (split_heads(q), split_heads(k), split_heads(v))
        attn = jax.nn.softmax(jnp.einsum('bhqd,bhkd->bhqk', q, k), axis=-1)
        o = jnp.einsum('bhqk,bhkd->bhqd', attn, v)
        o = o.transpose(0, 2, 1, 3).reshape(B, H * W, Cc)
        o = o @ wp.T + bp
        return o.transpose(0, 2, 1).reshape(B, Cc, H, W) + x

    def _L1_conv_ref(orig_batch, gn_w, gn_b, w1, b1, w2, b2):
        import jax, jax.numpy as jnp
        import numpy as np
        C = 128
        GROUPS = 32
        HEAD_CH = 16
        HEADS = C // HEAD_CH
        EPS = 1e-05
        B = orig_batch.shape[0]
        T = orig_batch.shape[2] * orig_batch.shape[3]
        xg = orig_batch.reshape(B, GROUPS, -1)
        mu = xg.mean(axis=-1, keepdims=True)
        var = xg.var(axis=-1, keepdims=True)
        xg = (xg - mu) * jax.lax.rsqrt(var + EPS)
        x = xg.reshape(B, C, T) * gn_w[None, :, None] + gn_b[None, :, None]
        qkv = jnp.einsum('oc,bct->bot', w1, x) + b1[None, :, None]
        q, k, v = jnp.split(qkv, 3, axis=1)
        q = q.reshape(B, HEADS, HEAD_CH, T)
        k = k.reshape(B, HEADS, HEAD_CH, T)
        v = v.reshape(B, HEADS, HEAD_CH, T)
        scale = 1.0 / np.sqrt(np.sqrt(HEAD_CH))
        w = jnp.einsum('bhct,bhcs->bhts', q * scale, k * scale)
        w = jax.nn.softmax(w, axis=-1)
        a = jnp.einsum('bhts,bhcs->bhct', w, v).reshape(B, C, T)
        out = jnp.einsum('oc,bct->bot', w2, a) + b2[None, :, None]
        return out.reshape(orig_batch.shape) + orig_batch

    def _L2_conv_ref(x, gn_weight, gn_bias, wq, bq, wkv, bkv, wproj, bproj):
        import jax, jax.numpy as jnp
        import numpy as np
        import math
        NUM_GROUPS = 32
        NUM_HEADS = 8
        EPS = 1e-05

        def _group_norm(x, weight, bias):
            b, c, h, w = x.shape
            xg = x.reshape(b, NUM_GROUPS, c // NUM_GROUPS, h, w)
            mean = jnp.mean(xg, axis=(2, 3, 4), keepdims=True)
            var = jnp.var(xg, axis=(2, 3, 4), keepdims=True)
            xn = ((xg - mean) * jax.lax.rsqrt(var + EPS)).reshape(b, c, h, w)
            return xn * weight[None, :, None, None] + bias[None, :, None, None]
        b, c, h, w = x.shape
        nh = NUM_HEADS
        hd = c // nh
        residual = x
        hs = _group_norm(x, gn_weight, gn_bias)
        hs = hs.reshape(b, c, h * w).transpose(0, 2, 1)
        q = hs @ wq.T + bq
        kv = hs @ wkv.T + bkv
        k, v = jnp.split(kv, 2, axis=2)

        def to_heads(t):
            return t.reshape(b, -1, nh, hd).transpose(0, 2, 1, 3)
        q, k, v = (to_heads(q), to_heads(k), to_heads(v))
        scale = 1.0 / math.sqrt(hd)
        scores = jnp.einsum('bhqd,bhkd->bhqk', q, k) * scale
        probs = jax.nn.softmax(scores.astype(jnp.float32), axis=-1).astype(scores.dtype)
        out = jnp.einsum('bhqk,bhkd->bhqd', probs, v)
        out = out.transpose(0, 2, 1, 3).reshape(b, h * w, c)
        out = out @ wproj.T + bproj
        out = out.transpose(0, 2, 1).reshape(b, c, h, w)
        return out + residual

    def _L3_conv_ref(x, gn_scale, gn_bias, qkv_w, qkv_b, proj_w, proj_b):
        import jax, jax.numpy as jnp
        import numpy as np
        NUM_GROUPS = 32
        EPS = 1e-06

        def _group_norm(x, scale, bias):
            b, c, h, w = x.shape
            xr = x.reshape(b, NUM_GROUPS, c // NUM_GROUPS, h, w)
            mean = xr.mean(axis=(2, 3, 4), keepdims=True)
            var = xr.var(axis=(2, 3, 4), keepdims=True)
            xn = ((xr - mean) * jax.lax.rsqrt(var + EPS)).reshape(b, c, h, w)
            return xn * scale[None, :, None, None] + bias[None, :, None, None]
        b, c, h, w = x.shape
        hw = h * w
        h_ = _group_norm(x, gn_scale, gn_bias)
        qkv = jnp.einsum('bchw,oc->bohw', h_, qkv_w) + qkv_b[None, :, None, None]
        q, k, v = jnp.split(qkv, 3, axis=1)
        q = q.reshape(b, c, hw).transpose(0, 2, 1)
        k = k.reshape(b, c, hw)
        v = v.reshape(b, c, hw)
        attn = jnp.einsum('bic,bcj->bij', q, k) * c ** (-0.5)
        attn = jax.nn.softmax(attn, axis=2)
        o = jnp.einsum('bcj,bij->bci', v, attn).reshape(b, c, h, w)
        o = jnp.einsum('bchw,oc->bohw', o, proj_w) + proj_b[None, :, None, None]
        return x + o

    def _gn(v, G=32, eps=1e-05):
        B_, C_, H_, W_ = v.shape
        g = v.reshape(B_, G, C_ // G, H_, W_)
        m = jnp.mean(g, axis=(2, 3, 4), keepdims=True)
        s = jnp.var(g, axis=(2, 3, 4), keepdims=True)
        return ((g - m) / jnp.sqrt(s + eps)).reshape(v.shape)

    def _ln_c(v, eps=1e-06):
        m = jnp.mean(v, axis=1, keepdims=True)
        s = jnp.var(v, axis=1, keepdims=True)
        return (v - m) / jnp.sqrt(s + eps)

    def _ln_t(v, eps=1e-05):
        m = jnp.mean(v, axis=-1, keepdims=True)
        s = jnp.var(v, axis=-1, keepdims=True)
        return (v - m) / jnp.sqrt(s + eps)

    def _to_tokens(v):
        B_, C_, H_, W_ = v.shape
        return v.reshape(B_, C_, H_ * W_).transpose(0, 2, 1)

    def _from_tokens(t, like):
        B_, C_, H_, W_ = like.shape
        return t.transpose(0, 2, 1).reshape(B_, C_, H_, W_)
    x = _L0_conv_ref(x, L0_conv_gn_w, L0_conv_gn_b, L0_conv_wq, L0_conv_bq, L0_conv_wk, L0_conv_bk, L0_conv_wv, L0_conv_bv, L0_conv_wp, L0_conv_bp)
    x = _L1_conv_ref(x, L1_conv_gn_w, L1_conv_gn_b, L1_conv_w1, L1_conv_b1, L1_conv_w2, L1_conv_b2)
    x = _L2_conv_ref(x, L2_conv_gn_weight, L2_conv_gn_bias, L2_conv_wq, L2_conv_bq, L2_conv_wkv, L2_conv_bkv, L2_conv_wproj, L2_conv_bproj)
    x = _L3_conv_ref(x, L3_conv_gn_scale, L3_conv_gn_bias, L3_conv_qkv_w, L3_conv_qkv_b, L3_conv_proj_w, L3_conv_proj_b)
    return x

_drawn_inputs = setup_inputs


def setup_inputs(seed=0):
    import zlib

    import numpy as np

    out = dict(_drawn_inputs(seed))
    spreads = {'L0_conv_gn_w': (1.0, 0.6),
     'L0_conv_gn_b': (0.0, 0.533),
     'L2_conv_gn_weight': (1.0, 0.6),
     'L2_conv_gn_bias': (0.0, 0.594),
     'L2_conv_bq': (0.0, 2.0),
     'L2_conv_bkv': (0.0, 0.665),
     'L2_conv_bproj': (0.0, 0.627),
     'L3_conv_gn_scale': (1.0, 0.6),
     'L3_conv_gn_bias': (0.0, 0.548),
     'L3_conv_qkv_b': (0.0, 0.702),
     'L3_conv_proj_b': (0.0, 0.657)}
    factors = {'L0_conv_wq': 8.0,
     'L0_conv_bq': 8.0,
     'L0_conv_wk': 8.0,
     'L0_conv_bk': 64.0,
     'L0_conv_wv': 3.696,
     'L0_conv_bv': 5.721,
     'L0_conv_wp': 2.883,
     'L1_conv_gn_w': 8.0,
     'L1_conv_b1': 3.966,
     'L1_conv_b2': 25.312,
     'L1_conv_gn_b': 3.703,
     'L2_conv_wq': 2.786}
    for name, (base, spread) in spreads.items():
        noise = np.random.default_rng([zlib.crc32(name.encode()), seed]).standard_normal(out[name].shape)
        drawn = base * np.exp(spread * noise) if base else spread * noise
        out[name] = jnp.asarray(drawn.astype(out[name].dtype))
    for name, factor in factors.items():
        out[name] = (out[name] * factor).astype(out[name].dtype)
    return out
```

```python
from contextlib import ExitStack

import concourse.bass as bass
from concourse import mybir

F32 = mybir.dt.float32
F32R = mybir.dt.float32r
ACT = mybir.ActivationFunctionType
ALU = mybir.AluOpType
AX_X = mybir.AxisListType.X

B, C, T = 2, 128, 256
HEADS, DH = 8, 16
STACKS, PER = 2, 4
QUAD = 32
MULTI = 3
BLOCKS = 4
CHUNK = 128
NCH = T // CHUNK
GROUP = 4
EPS = [1e-5, 1e-5, 1e-5, 1e-6]
SCALE = DH ** -0.5
SCALE_ONE = C ** -0.5
SLOTS = 2

GN_W, GN_B, BQ, BK, BV, BP = 0, 1, 2, 4, 6, 7
NVEC = 8
W_MULTI = 2 * STACKS * C + 2 * C
W_ONE = 4 * C
NCONST = 2 * C + PER * C + 2

def chain(l, b, t):
    s = []

    def step(at, kind, i=0):
        s.append((at, kind, l, b, i))

    step(t, "moments")
    step(t + 0.6, "group_means")
    step(t + 1.2, "variance")
    step(t + 1.6, "rsqrt")
    step(t + 2.1, "normalise")
    t += 2.9
    step(t, "project_q")
    step(t + 0.9, "project_k")
    step(t + 1.0, "store_q")
    step(t + 1.9, "store_k")
    step(t + 1.8, "project_v")
    step(t + 1.8, "split_q")
    step(t + 2.9, "store_v")
    if l < MULTI:
        step(t + 2.8, "mask_q")
        step(t + 3.5, "split_k")
        t += 4.0
        for h in range(HEADS):
            step(t + 0.65 * h, "scores", h)
            step(t + 0.65 * h + 0.35, "row_max", h)
        for half in range(STACKS):
            u = t + 0.65 * PER * (half + 1) + 0.3
            step(u, "turn_max", half)
            step(u + 0.3, "store_max", half)
        t += 0.65 * PER + 1.2
        for h in range(HEADS):
            step(t + 0.6 * h, "scores_t", h)
            step(t + 0.6 * h + 0.5, "exps", h)
        for half in range(STACKS):
            step(t + 0.6 * PER * (half + 1) + 0.9, "attend", half)
        t += 0.6 * HEADS + 2.0
        step(t, "store_out")
        step(t + 0.6, "turn_out")
        step(t + 1.3, "divide")
        step(t + 2.1, "turn_back")
        t += 2.5
    else:
        t += 2.5
        step(t, "scores", 0)
        step(t + 1.0, "row_max", 0)
        step(t + 1.6, "exps", 0)
        step(t + 2.6, "divide")
        step(t + 3.4, "turn_p")
        step(t + 4.0, "store_p")
        step(t + 4.6, "attend", 0)
        t += 5.6
    step(t, "store_attended")
    step(t + 0.4, "project_out")
    step(t + 1.0, "residual")
    if l == BLOCKS - 1:
        step(t + 1.4, "write")
    return s, t + 1.6


def build_order(lag):
    order = []
    for b in range(B):
        t = b * lag
        for l in range(BLOCKS):
            steps, t = chain(l, b, t)
            order += steps
    order.sort(key=lambda s: s[0])
    return [s[1:] for s in order]


def attention_blocks(nc: bass.Bass, x, out, vectors, constants, weights):
    order = build_order(11.0)
    count, seen = {}, {}
    for kind, l, b, i in order:
        seen[kind] = seen.get(kind, 0) + 1
        count[kind, l, b, i] = seen[kind]

    def nth(kind, l, b, i=0):
        return count[kind, l, b, i]

    def before(kind, step):
        return sum(1 for s in order[:order.index(step)] if s[0] == kind)

    with ExitStack() as ctx:
        def sb(name, shape, dt=F32):
            return ctx.enter_context(nc.sbuf_tensor(name, shape, dt))

        def sem(name):
            return ctx.enter_context(nc.semaphore(name))

        xs = [sb(f"xs{b}", [C, T]) for b in range(B)]
        vec = sb("vec", [C, BLOCKS, NVEC])
        const = sb("const", [C, NCONST])
        w = [sb(f"w{l}", [C, W_MULTI if l < MULTI else W_ONE]) for l in range(BLOCKS)]
        ident = const[:, 0:C]
        group_avg = const[:, C:2 * C]
        minus_low_rows = const[:, NCONST - 2:NCONST - 1]
        minus_half = const[:, NCONST - 1:NCONST]
        head_row = sb("head_row", [PER, PER, C], F32R)

        bn = [sb(f"bn{b}", [C, 6]) for b in range(B)]
        mom = [sb(f"mom{b}", [C, 3]) for b in range(B)]
        grp = [sb(f"grp{b}", [C, 7]) for b in range(B)]
        hn = [sb(f"hn{b}", [C, T]) for b in range(B)]
        q32 = [sb(f"q32_{b}", [C, STACKS, T]) for b in range(B)]
        q_round = [sb(f"q_round{b}", [C, STACKS, T], F32R) for b in range(B)]
        q_parts = [sb(f"q_parts{b}", [C, STACKS, T], F32R) for b in range(B)]
        q_heads = [sb(f"q_heads{b}", [C, HEADS, T], F32R) for b in range(B)]
        k_high = [sb(f"k_high{b}", [C, STACKS, T], F32R) for b in range(B)]
        k32 = [sb(f"k32_{b}", [C, STACKS, T]) for b in range(B)]
        k_low = [sb(f"k_low{b}", [C, STACKS, T], F32R) for b in range(B)]
        v_heads = [sb(f"v_heads{b}", [C, NCH, HEADS, 2 * DH]) for b in range(B)]
        v_one = [sb(f"v_one{b}", [C, NCH, C]) for b in range(B)]
        neg_max = [sb(f"neg_max{b}", [C, STACKS, NCH, PER]) for b in range(B)]
        neg_max_s = [sb(f"neg_max_s{b}", [C, NCH]) for b in range(B)]
        max_rows = [sb(f"max_rows{b}", [PER, STACKS, T], F32R) for b in range(B)]
        probs = sb("probs", [C, HEADS, NCH, T])
        p_one = [sb(f"p_one{b}", [C, NCH, T]) for b in range(B)]
        pt_one = [sb(f"pt_one{b}", [C, NCH, T]) for b in range(B)]
        sums = [sb(f"sums{b}", [C, NCH]) for b in range(B)]
        o_raw = [sb(f"o_raw{b}", [C, STACKS, T]) for b in range(B)]
        rden = [sb(f"rden{b}", [C, HEADS * NCH]) for b in range(B)]
        o_tok = [sb(f"o_tok{b}", [C, NCH, C]) for b in range(B)]
        att = [sb(f"att{b}", [C, T]) for b in range(B)]

        def bank(name):
            return ctx.enter_context(nc.psum_tensor(name, [C, 512], F32))

        ps_s = [bank(f"ps_s{i}") for i in range(SLOTS)]
        ps_t = [bank(f"ps_t{i}") for i in range(SLOTS)]
        ps_m = [bank(f"ps_m{b}") for b in range(B)]
        ps_k = bank("ps_k")
        ps_o = bank("ps_o")

        x_in = [sem(f"x_in{b}") for b in range(B)]
        const_in = sem("const_in")
        w_in = [sem(f"w_in{l}") for l in range(BLOCKS)]
        out_written = sem("out_written")
        zeros_ready = sem("zeros_ready")
        v_ones_ready = sem("v_ones_ready")
        vchain = sem("vchain")
        head_rows_ready = sem("head_rows_ready")
        moments_done = sem("moments_done")
        means_done = sem("means_done")
        variance_ready, rsqrt_ready, h_ready = sem("variance_ready"), sem("rsqrt_ready"), sem("h_ready")
        q_projected, k_projected, v_projected = sem("q_projected"), sem("k_projected"), sem("v_projected")
        q_stored, k_stored, v_stored = sem("q_stored"), sem("k_stored"), sem("v_stored")
        q_split, k_split = sem("q_split"), sem("k_split")
        q_masked_v, q_masked_a = sem("q_masked_v"), sem("q_masked_a")
        scores_done, max_done = sem("scores_done"), sem("max_done")
        max_turned, max_stored = sem("max_turned"), sem("max_stored")
        scores_t_done, exps_done, attended = sem("scores_t_done"), sem("exps_done"), sem("attended")
        out_stored, out_turned, divided, out_back = (sem("out_stored"), sem("out_turned"), sem("divided"),
                                                     sem("out_back"))
        p_turned, p_stored = sem("p_turned"), sem("p_stored")
        att_stored, out_projected, x_ready = sem("att_stored"), sem("out_projected"), sem("x_ready")

        s_slot = {s: n % SLOTS for n, s in enumerate(s for s in order if s[0] == "scores")}
        t_users = [s for s in order if s[0] in ("scores_t", "turn_p")]
        t_slot = {s: n % SLOTS for n, s in enumerate(t_users)}

        block = ctx.enter_context(nc.Block())

        @block.sync
        def _(sp):
            sp.dma_start(xs[0][:, :], x[0]).then_inc(x_in[0], 16)
            sp.dma_start(const[:, :], constants).then_inc(const_in, 16)
            sp.dma_start(vec[:, :, :], vectors).then_inc(const_in, 16)
            sp.dma_start(w[0][:, :], weights[0]).then_inc(w_in[0], 16)
            sp.dma_start(xs[1][:, :], x[1]).then_inc(x_in[1], 16)
            for l in range(1, BLOCKS):
                sp.dma_start(w[l][:, :], weights[l]).then_inc(w_in[l], 16)
            for step in order:
                kind, l, b, i = step
                if kind == "write":
                    sp.wait_ge(x_ready, nth("residual", l, b))
                    sp.dma_start(out[b], xs[b][:, :]).then_inc(out_written, 16)
            sp.wait_ge(out_written, 16 * B)

        @block.gpsimd
        def _(pool):
            for b in range(B):
                nc.gpsimd.memset(q_heads[b][:, :, :].bitcast(F32), 0.0).then_inc(zeros_ready, 1)
                nc.gpsimd.memset(v_heads[b][:, :, :, :], 1.0).then_inc(v_ones_ready, 1)
            pool.wait_ge(const_in, 32)
            for kind, l, b, i in order:
                if kind == "rsqrt":
                    pool.wait_ge(variance_ready, nth("variance", l, b))
                    nc.gpsimd.tensor_tensor(grp[b][:, 6:7], grp[b][:, 3:4], minus_half,
                                            ALU.pow).then_inc(rsqrt_ready, 1)

        @block.tensor
        def _(pe):
            mm = nc.tensor.matmul
            for step in order:
                kind, l, b, i = step
                multi = l < MULTI
                m = ps_m[b]
                if kind == "group_means":
                    if l == 0:
                        pe.wait_ge(const_in, 32)
                    pe.wait_ge(moments_done, nth("moments", l, b))
                    mm(m[:, 0:2], group_avg, mom[b][:, 0:3:2], start=True, stop=True).then_inc(means_done, 1)
                elif kind == "project_q":
                    pe.wait_ge(w_in[l], 16)
                    pe.wait_ge(h_ready, nth("normalise", l, b))
                    for n in range(2):
                        last = mm(m[:, n * T:(n + 1) * T], w[l][:, n * C:(n + 1) * C], hn[b][:, :],
                                  start=True, stop=True)
                    last.then_inc(q_projected, 1)
                elif kind == "project_k" and multi:
                    done = before("store_k", step)
                    if done:
                        pe.wait_ge(k_stored, done)
                    for n in range(STACKS):
                        last = mm(ps_k[:, n * T:(n + 1) * T], w[l][:, (2 + n) * C:(3 + n) * C], hn[b][:, :],
                                  start=True, stop=True)
                    last.then_inc(k_projected, 1)
                elif kind == "project_v":
                    pe.wait_ge(q_stored, nth("store_q", l, b))
                    at = (4 if multi else 2) * C
                    for n in range(NCH):
                        last = mm(m[:, n * C:(n + 1) * C], hn[b][:, n * CHUNK:(n + 1) * CHUNK],
                                  w[l][:, at:at + C], start=True, stop=True)
                    last.then_inc(v_projected, 1)
                elif kind == "scores":
                    slot = s_slot[step]
                    n = nth(*step)
                    if n > SLOTS:
                        pe.wait_ge(max_done, n - SLOTS)
                    if multi and i == 0:
                        pe.wait_ge(q_masked_v, nth("mask_q", l, b))
                        pe.wait_ge(q_masked_a, nth("mask_q", l, b))
                        pe.wait_ge(k_stored, nth("store_k", l, b))
                    for qc in range(NCH):
                        cols = slice(qc * CHUNK, (qc + 1) * CHUNK)
                        lhs = q_heads[b][:, i, cols] if multi else q32[b][:, 0, cols]
                        rhs = k_high[b][:, i // PER, :] if multi else q32[b][:, 1, :]
                        last = mm(ps_s[slot][:, qc * T:(qc + 1) * T], lhs, rhs, start=True, stop=True)
                    last.then_inc(scores_done, 1)
                elif kind == "turn_max":
                    pe.wait_ge(max_done, nth("row_max", l, b, PER * (i + 1) - 1))
                    if i == 0:
                        pe.wait_ge(v_stored, nth("store_v", l, b))
                    else:
                        pe.wait_ge(max_stored, nth("store_max", l, b, 0))
                    for qc in range(NCH):
                        last = nc.tensor.transpose(m[0:PER, qc * CHUNK:(qc + 1) * CHUNK], neg_max[b][:, i, qc, :],
                                                   ident)
                    last.then_inc(max_turned, 1)
                elif kind == "scores_t":
                    if i % PER == 0:
                        pe.wait_ge(max_stored, nth("store_max", l, b, i // PER))
                    if i == 0:
                        pe.wait_ge(k_split, nth("split_k", l, b))
                        pe.wait_ge(head_rows_ready, 1)
                    n = t_users.index(step)
                    if n >= SLOTS:
                        pe.wait_ge(exps_done, nth("exps", *t_users[n - SLOTS][1:]))
                    for kc in range(NCH):
                        dst = ps_t[t_slot[step]][:, kc * T:(kc + 1) * T]
                        keys = slice(kc * CHUNK, (kc + 1) * CHUNK)
                        mm(dst, k_high[b][:, i // PER, keys], q_heads[b][:, i, :], start=True, stop=False)
                        mm(dst, k_low[b][:, i // PER, keys], q_heads[b][:, i, :], start=False, stop=False)
                        last = mm(dst, head_row[:, i % PER, :], max_rows[b][:, i // PER, :], start=False, stop=True)
                    last.then_inc(scores_t_done, 1)
                elif kind == "attend" and multi:
                    pe.wait_ge(exps_done, nth("exps", l, b, PER * (i + 1) - 1))
                    if l == 0 and i == 0:
                        pe.wait_ge(v_ones_ready, b + 1)
                    pe.wait_ge(v_stored, nth("store_v", l, b))
                    done = before("store_out", step)
                    if i == 0 and done:
                        pe.wait_ge(out_stored, done)
                    for kc in range(NCH):
                        for j in range(PER):
                            h = PER * i + j
                            last = mm(ps_o[QUAD * j:QUAD * (j + 1), i * T:(i + 1) * T], v_heads[b][:, kc, h, :],
                                      probs[:, h, kc, :], start=(kc == 0), stop=(kc == NCH - 1))
                    last.then_inc(attended, 1)
                elif kind == "attend":
                    pe.wait_ge(p_stored, nth("store_p", l, b))
                    pe.wait_ge(v_stored, nth("store_v", l, b))
                    for kc in range(NCH):
                        last = mm(m[:, 0:T], v_one[b][:, kc, :], pt_one[b][:, kc, :],
                                  start=(kc == 0), stop=(kc == NCH - 1))
                    last.then_inc(attended, 1)
                elif kind == "turn_p":
                    pe.wait_ge(divided, nth("divide", l, b))
                    n = t_users.index(step)
                    prev = t_users[n - SLOTS]
                    if prev[0] == "scores_t":
                        pe.wait_ge(exps_done, nth("exps", *prev[1:]))
                    else:
                        pe.wait_ge(p_stored, nth("store_p", *prev[1:3]))
                    for kc in range(NCH):
                        for qc in range(NCH):
                            at = kc * T + qc * CHUNK
                            last = nc.tensor.transpose(ps_t[t_slot[step]][:, at:at + CHUNK],
                                                       p_one[b][:, qc, kc * CHUNK:(kc + 1) * CHUNK], ident)
                    last.then_inc(p_turned, 1)
                elif kind == "turn_out":
                    pe.wait_ge(out_stored, nth("store_out", l, b))
                    for qc in range(NCH):
                        for s in range(STACKS):
                            at = (qc * STACKS + s) * C
                            last = nc.tensor.transpose(m[:, at:at + C],
                                                       o_raw[b][:, s, qc * CHUNK:(qc + 1) * CHUNK], ident)
                    last.then_inc(out_turned, 1)
                elif kind == "turn_back":
                    pe.wait_ge(divided, nth("divide", l, b))
                    for qc in range(NCH):
                        last = nc.tensor.transpose(m[:, qc * CHUNK:(qc + 1) * CHUNK], o_tok[b][:, qc, :], ident)
                    last.then_inc(out_back, 1)
                elif kind == "project_out":
                    pe.wait_ge(att_stored, nth("store_attended", l, b))
                    at = (5 if multi else 3) * C
                    mm(m[:, 0:T], w[l][:, at:at + C], att[b][:, :], start=True, stop=True).then_inc(out_projected, 1)

        @block.scalar
        def _(act):
            act.wait_ge(const_in, 32)
            for step in order:
                kind, l, b, i = step
                multi = l < MULTI
                m = ps_m[b]
                if kind == "store_q":
                    act.wait_ge(q_projected, nth("project_q", l, b))
                    for n in range(2):
                        col = BQ + n if multi else (BQ, BK)[n]
                        last = nc.scalar.activation(q32[b][:, n, :], m[:, n * T:(n + 1) * T], ACT.Identity,
                                                    bias=vec[:, l, col:col + 1])
                    last.then_inc(q_stored, 1)
                elif kind == "store_k" and multi:
                    act.wait_ge(k_projected, nth("project_k", l, b))
                    for n in range(STACKS):
                        src = ps_k[:, n * T:(n + 1) * T]
                        nc.scalar.activation(k_high[b][:, n, :], src, ACT.Identity,
                                             bias=vec[:, l, BK + n:BK + n + 1])
                        last = nc.scalar.activation(k32[b][:, n, :], src, ACT.Identity,
                                                    bias=vec[:, l, BK + n:BK + n + 1])
                    last.then_inc(k_stored, 1)
                elif kind == "store_v":
                    act.wait_ge(v_projected, nth("project_v", l, b))
                    if multi:
                        if l == 0:
                            act.wait_ge(v_ones_ready, b + 1)
                        dst = v_heads[b][:, :, :, 0:DH].rearrange("p c h d -> p (c h) d")
                        src = m[:, 0:NCH * C].rearrange("p (c d) -> p c d", d=DH)
                    else:
                        dst = v_one[b][:, :, :].rearrange("p c d -> p (c d)")
                        src = m[:, 0:NCH * C]
                    nc.scalar.activation(dst, src, ACT.Copy).then_inc(v_stored, 1)
                elif kind == "mask_q":
                    act.wait_ge(q_split, nth("split_q", l, b))
                    if l == 0:
                        act.wait_ge(zeros_ready, b + 1)
                    for j in range(2, PER):
                        rows = slice(QUAD * j, QUAD * (j + 1))
                        last = nc.scalar.activation(q_heads[b][rows, j:HEADS:PER, :], q_parts[b][rows, :, :], ACT.Copy)
                    last.then_inc(q_masked_a, 1)
                elif kind == "store_max":
                    act.wait_ge(max_turned, nth("turn_max", l, b, i))
                    nc.scalar.activation(max_rows[b][:, i, :], m[0:PER, 0:T],
                                         ACT.Copy).then_inc(max_stored, 1)
                elif kind == "exps" and multi:
                    act.wait_ge(scores_t_done, nth("scores_t", l, b, i))
                    done = before("attend", step)
                    if done >= STACKS and i % PER == 0:
                        act.wait_ge(attended, done - 1)
                    src = ps_t[t_slot["scores_t", l, b, i]][:, :]
                    nc.scalar.activation(probs[:, i, :, :].rearrange("p c t -> p (c t)"), src, ACT.Exp,
                                         scale=SCALE).then_inc(exps_done, 1)
                elif kind == "exps":
                    act.wait_ge(max_done, nth("row_max", l, b, 0))
                    for qc in range(NCH):
                        src = ps_s[s_slot["scores", l, b, 0]][:, qc * T:(qc + 1) * T]
                        last = nc.scalar.activation(p_one[b][:, qc, :], src, ACT.Exp, scale=SCALE_ONE,
                                                    bias=neg_max_s[b][:, qc:qc + 1],
                                                    accum_out=sums[b][:, qc:qc + 1])
                    last.then_inc(exps_done, 1)
                elif kind == "store_p":
                    act.wait_ge(p_turned, nth("turn_p", l, b))
                    nc.scalar.activation(pt_one[b][:, :, :].rearrange("p c t -> p (c t)"),
                                         ps_t[t_slot["turn_p", l, b, 0]][:, :], ACT.Copy).then_inc(p_stored, 1)
                elif kind == "store_out":
                    act.wait_ge(attended, nth("attend", l, b, STACKS - 1))
                    nc.scalar.activation(o_raw[b][:, :, :].rearrange("p s t -> p (s t)"), ps_o[:, :],
                                         ACT.Copy).then_inc(out_stored, 1)
                elif kind == "store_attended":
                    if multi:
                        act.wait_ge(out_back, nth("turn_back", l, b))
                    else:
                        act.wait_ge(attended, nth("attend", l, b, 0))
                    nc.scalar.activation(att[b][:, :], m[:, 0:T], ACT.Identity,
                                         bias=vec[:, l, BV:BV + 1]).then_inc(att_stored, 1)

        @block.vector
        def _(dve):
            links = [0]

            def link(ins):
                links[0] += 1
                ins.then_inc(vchain, 1)
                dve.wait_ge(vchain, links[0])

            tt, ts, stt = nc.vector.tensor_tensor, nc.vector.tensor_scalar, nc.vector.scalar_tensor_tensor
            for step in order:
                kind, l, b, i = step
                multi = l < MULTI
                m = ps_m[b]
                if kind == "moments":
                    if l == 0:
                        dve.wait_ge(x_in[b], 16)
                    else:
                        dve.wait_ge(x_ready, nth("residual", l - 1, b))
                    link(nc.vector.bn_stats(bn[b][:, :], xs[b][:, :]))
                    link(nc.vector.bn_aggr(mom[b][:, 0:2], bn[b][:, :]))
                    stt(out=mom[b][:, 2:3], in0=mom[b][:, 0:1], scalar=mom[b][:, 0:1], in1=mom[b][:, 1:2],
                        op0=ALU.mult, op1=ALU.add).then_inc(moments_done, 1)
                elif kind == "variance":
                    g = grp[b]
                    if l == 0:
                        dve.wait_ge(const_in, 32)
                        if b == 0:
                            nc.vector.tensor_copy(head_row[:, :, :].rearrange("p j c -> p (j c)"),
                                                  const[0:PER, 2 * C:2 * C + PER * C]).then_inc(head_rows_ready, 1)
                    dve.wait_ge(means_done, nth("group_means", l, b))
                    link(nc.vector.tensor_copy(g[:, 0:2], m[:, 0:2]))
                    link(stt(out=g[:, 2:3], in0=g[:, 0:1], scalar=g[:, 0:1], in1=g[:, 1:2],
                             op0=ALU.mult, op1=ALU.subtract))
                    ts(g[:, 3:4], g[:, 2:3], -1.0, EPS[l], ALU.mult, ALU.add).then_inc(variance_ready, 1)
                elif kind == "normalise":
                    g = grp[b]
                    dve.wait_ge(rsqrt_ready, nth("rsqrt", l, b))
                    link(ts(g[:, 4:5], g[:, 6:7], vec[:, l, GN_W:GN_W + 1], None, ALU.mult))
                    link(stt(out=g[:, 5:6], in0=g[:, 0:1], scalar=g[:, 4:5], in1=vec[:, l, GN_B:GN_B + 1],
                             op0=ALU.mult, op1=ALU.subtract))
                    ts(hn[b][:, :], xs[b][:, :], g[:, 4:5], g[:, 5:6], ALU.mult, ALU.subtract).then_inc(h_ready, 1)
                elif kind == "split_q" and multi:
                    dve.wait_ge(q_stored, nth("store_q", l, b))
                    link(nc.vector.tensor_copy(q_round[b][:, :, :], q32[b][:, :, :]))
                    stt(out=q_parts[b][:, :, :], in0=q_round[b][:, :, :].bitcast(F32), scalar=minus_low_rows,
                        in1=q32[b][:, :, :], op0=ALU.mult, op1=ALU.add).then_inc(q_split, 1)
                elif kind == "mask_q":
                    dve.wait_ge(q_split, nth("split_q", l, b))
                    if l == 0:
                        dve.wait_ge(zeros_ready, b + 1)
                    for j in range(0, 2):
                        rows = slice(QUAD * j, QUAD * (j + 1))
                        last = nc.vector.tensor_copy(q_heads[b][rows, j:HEADS:PER, :], q_parts[b][rows, :, :])
                    last.then_inc(q_masked_v, 1)
                elif kind == "split_k":
                    dve.wait_ge(k_stored, nth("store_k", l, b))
                    tt(k_low[b][:, :, :], k32[b][:, :, :], k_high[b][:, :, :].bitcast(F32),
                       ALU.subtract).then_inc(k_split, 1)
                elif kind == "row_max":
                    dve.wait_ge(scores_done, nth("scores", l, b, i))
                    src = ps_s[s_slot["scores", l, b, i]][:, :].rearrange("p (c t) -> p c t", c=NCH)
                    red = nc.vector.tensor_reduce(neg_max[b][:, i // PER, :, i % PER], src, AX_X, ALU.max,
                                                  negate=True)
                    if multi:
                        red.then_inc(max_done, 1)
                    else:
                        link(red)
                        ts(neg_max_s[b][:, :], neg_max[b][:, 0, :, 0], SCALE_ONE, None, ALU.mult).then_inc(max_done, 1)
                elif kind == "divide" and multi:
                    dve.wait_ge(out_turned, nth("turn_out", l, b))
                    src = m[:, :].rearrange("p (n e) -> p n e", e=2 * DH)
                    link(nc.vector.reciprocal(rden[b][:, :], src[:, :, DH:DH + 1].rearrange("p n e -> p (n e)")))
                    tt(o_tok[b][:, :, :].rearrange("p c (h d) -> p (c h) d", d=DH), src[:, :, 0:DH],
                       rden[b][:, :].unsqueeze(2).to_broadcast([C, HEADS * NCH, DH]), ALU.mult).then_inc(divided, 1)
                elif kind == "divide":
                    dve.wait_ge(exps_done, nth("exps", l, b, 0))
                    link(nc.vector.reciprocal(rden[b][:, 0:NCH], sums[b][:, :]))
                    for qc in range(NCH):
                        last = ts(p_one[b][:, qc, :], p_one[b][:, qc, :], rden[b][:, qc:qc + 1], None, ALU.mult)
                    last.then_inc(divided, 1)
                elif kind == "residual":
                    dve.wait_ge(out_projected, nth("project_out", l, b))
                    stt(out=xs[b][:, :], in0=m[:, 0:T], scalar=vec[:, l, BP:BP + 1], in1=xs[b][:, :],
                        op0=ALU.add, op1=ALU.add).then_inc(x_ready, 1)


def kernel(**inputs):
    import numpy as np
    import concourse.bacc as bacc
    from concourse.bass_utils import run_bass_kernel_spmd

    a = {k: np.asarray(v) for k, v in inputs.items()}
    row = np.arange(C)
    chan = row // QUAD * DH + row % DH
    high = row % QUAD < DH
    wq, wk, wv, wp = {}, {}, {}, {}
    bq, bk, bv, bp, gw, gb = {}, {}, {}, {}, {}, {}
    p = "L0_conv_"
    wq[0], wk[0], wv[0], wp[0] = (a[p + n] for n in ("wq", "wk", "wv", "wp"))
    bq[0], bk[0], bv[0], bp[0] = (a[p + n] for n in ("bq", "bk", "bv", "bp"))
    gw[0], gb[0] = a[p + "gn_w"], a[p + "gn_b"]
    p = "L1_conv_"
    wq[1], wk[1], wv[1] = (a[p + "w1"][n * C:(n + 1) * C] for n in range(3))
    bq[1], bk[1], bv[1] = (a[p + "b1"][n * C:(n + 1) * C] for n in range(3))
    wp[1], bp[1], gw[1], gb[1] = a[p + "w2"], a[p + "b2"], a[p + "gn_w"], a[p + "gn_b"]
    p = "L2_conv_"
    wq[2], bq[2], wp[2], bp[2] = a[p + "wq"], a[p + "bq"], a[p + "wproj"], a[p + "bproj"]
    wk[2], wv[2] = (a[p + "wkv"][n * C:(n + 1) * C] for n in range(2))
    bk[2], bv[2] = (a[p + "bkv"][n * C:(n + 1) * C] for n in range(2))
    gw[2], gb[2] = a[p + "gn_weight"], a[p + "gn_bias"]
    p = "L3_conv_"
    wq[3], wk[3], wv[3] = (a[p + "qkv_w"][n * C:(n + 1) * C] for n in range(3))
    bq[3], bk[3], bv[3] = (a[p + "qkv_b"][n * C:(n + 1) * C] for n in range(3))
    wp[3], bp[3], gw[3], gb[3] = a[p + "proj_w"], a[p + "proj_b"], a[p + "gn_scale"], a[p + "gn_bias"]

    vectors = np.zeros((C, BLOCKS, NVEC), np.float32)
    arrays = {"x": np.ascontiguousarray(a["x"].reshape(B, C, T))}
    for l in range(BLOCKS):
        if l < MULTI:
            cols = []
            for m, bias, at in ((wq[l], bq[l], BQ), (wk[l], bk[l], BK)):
                for s in range(STACKS):
                    cols.append(m[s * C // 2 + chan].T)
                    vectors[:, l, at + s] = bias[s * C // 2 + chan]
        else:
            cols = [wq[l].T, wk[l].T]
            vectors[:, l, BQ], vectors[:, l, BK] = bq[l], bk[l]
        arrays[f"w{l}"] = np.ascontiguousarray(np.concatenate(cols + [wv[l].T, wp[l].T], axis=1))
        for at, v in ((GN_W, gw), (GN_B, gb), (BV, bv), (BP, bp)):
            vectors[:, l, at] = v[l]
    arrays["vectors"] = vectors
    constants = np.zeros((C, NCONST), np.float32)
    constants[:, 0:C] = np.eye(C)
    constants[:, C:2 * C] = np.kron(np.eye(C // GROUP), np.full((GROUP, GROUP), 1.0 / GROUP))
    constants[0:PER, 2 * C:(2 + PER) * C] = np.kron(np.eye(PER), np.ones((1, C)))
    constants[:, NCONST - 2] = np.where(high, 0.0, -1.0)
    constants[:, NCONST - 1] = -0.5
    arrays["constants"] = constants

    nc = bacc.Bacc("TRN2", target_bir_lowering=False, num_devices=1)
    ap = {n: nc.dram_tensor(f"in_{n}", v.shape, mybir.dt.float32, kind="ExternalInput").ap() for n, v in arrays.items()}
    out = nc.dram_tensor("out", (B, C, T), mybir.dt.float32, kind="ExternalOutput").ap()
    attention_blocks(nc, ap["x"], out, ap["vectors"], ap["constants"], [ap[f"w{l}"] for l in range(BLOCKS)])
    r = run_bass_kernel_spmd(nc, [{f"in_{n}": v for n, v in arrays.items()}], core_ids=[0])
    return r.results[0]["out"].reshape(a["x"].shape)
```

```python
from contextlib import ExitStack

import concourse.bass as bass
from concourse import mybir

F32 = mybir.dt.float32
F32R = mybir.dt.float32r
ACT = mybir.ActivationFunctionType
ALU = mybir.AluOpType
AX_X = mybir.AxisListType.X

B, C, T = 2, 128, 256
HEADS, DH = 8, 16
STACKS, PER = 2, 4
QUAD = 32
PAIRS = HEADS // 2
HALF = C // 2
MULTI = 3
BLOCKS = 4
CHUNK = 128
NCH = T // CHUNK
GROUP = 4
EPS = [1e-5, 1e-5, 1e-5, 1e-6]
SCALE = DH ** -0.5
SCALE_ONE = C ** -0.5
WORK, SLOTS = 3, 2

GN_W, GN_B, BQ, BK, BV, BP = range(6)
NVEC = 6
SEL = 2 * C
SELS = 4
PAIR_COL = SEL + SELS * C
ROWS = PAIR_COL + PAIRS
HALF_COL = ROWS + 2 * C
NCONST = HALF_COL + 1

STEPS = {
    "moments": {"V": .79}, "group_means": {"P": .1}, "variance": {"V": .39}, "rsqrt": {"G": .5},
    "normalise": {"V": .89}, "project": {"P": .43}, "round": {"A": .36}, "split": {"V": .4},
    "project_v": {"P": .43}, "store_v": {"A": .27}, "place_q": {"P": .44}, "place_k": {"P": .44},
    "store_q": {"A": .48, "V": .6}, "store_k": {"A": .57}, "scores": {"P": .22}, "row_max": {"V": .6},
    "turn_max": {"P": .22}, "store_max": {"A": .26}, "scores_t": {"P": .44}, "exps": {"A": .48},
    "attend": {"P": 1.01}, "store_out": {"A": .27}, "turn_out": {"P": .22}, "divide": {"V": .44},
    "turn_back": {"P": .22}, "store_attended": {"A": .36}, "project_out": {"P": .43}, "residual": {"V": .4},
}
ONE_HEAD_STEPS = {
    "scores": {"P": .86}, "row_max": {"V": .75}, "exps": {"A": 1.}, "divide": {"V": .85}, "turn_p": {"P": .5},
    "store_p": {"A": .48}, "attend": {"P": .86}, "write": {"S": .1},
}
HANDOVER = {"P": .2, "A": .3, "V": .2, "G": .1, "S": 2.}
READ_BY = {"project": "split", "place_q": "store_q", "place_k": "store_k", "scores": "row_max",
           "scores_t": "exps", "turn_p": "store_p"}
READ_BY_ONE_HEAD = {**READ_BY, "project": "round", "scores": "exps"}
RING_W = ("project", "place_q", "place_k", "scores")
RING_T = ("scores_t", "turn_p")
LEAD = 8.
FAVOURED = {}


def step_needs():
    needs = {}
    for b in range(B):
        for l in range(BLOCKS):
            def step(kind, i, *others):
                needs[kind, l, b, i] = [(k, l, b, j) for k, j in others]

            step("moments", 0)
            if l > 0:
                needs["moments", l, b, 0] = [("residual", l - 1, b, 0)]
            step("group_means", 0, ("moments", 0))
            step("variance", 0, ("group_means", 0))
            step("rsqrt", 0, ("variance", 0))
            step("normalise", 0, ("rsqrt", 0))
            for n in range(2):
                step("project", n, ("normalise", 0), *[("project", 0)] * n)
                step("round", n, ("project", n))
                if l < MULTI:
                    step("split", n, ("round", n))
            step("project_v", 0, ("normalise", 0))
            step("store_v", 0, ("project_v", 0))
            if l < MULTI:
                for n in range(STACKS):
                    step("place_q", n, ("split", 0), *[("place_k", n - 1)] * n)
                    step("place_k", n, ("split", 1), ("place_q", n))
                    step("store_q", n, ("place_q", n))
                    step("store_k", n, ("place_k", n))
                    step("attend", n, ("store_v", 0), *[("exps", PER * n + j) for j in range(PER)],
                         *[("store_out", n - 1)] * n)
                    step("store_out", n, ("attend", n))
                    step("turn_out", n, ("store_out", n), ("store_max", PAIRS - 1), *[("divide", n - 1)] * n)
                    step("divide", n, ("turn_out", n))
                for n in range(PAIRS):
                    step("turn_max", n, ("store_v", 0), ("row_max", 2 * n), ("row_max", 2 * n + 1),
                         *[("store_max", n - 1)] * min(n, 1))
                    step("store_max", n, ("turn_max", n))
                for h in range(HEADS):
                    after = [("scores", h - 1), ("row_max", h - 1), ("scores_t", h - 1), ("exps", h - 1)] * min(h, 1)
                    step("scores", h, ("store_q", h // PER), ("store_k", h // PER), *after[0:1])
                    step("row_max", h, ("scores", h), *after[1:2])
                    step("scores_t", h, ("store_max", h // 2), *after[2:3])
                    step("exps", h, ("scores_t", h), *after[3:4])
                step("turn_back", 0, ("divide", STACKS - 1))
                step("store_attended", 0, ("turn_back", 0))
            else:
                step("scores", 0, ("round", 1))
                step("row_max", 0, ("scores", 0))
                step("exps", 0, ("row_max", 0))
                step("divide", 0, ("exps", 0))
                step("turn_p", 0, ("divide", 0))
                step("store_p", 0, ("turn_p", 0))
                step("attend", 0, ("store_p", 0), ("store_v", 0))
                step("store_attended", 0, ("attend", 0))
                step("write", 0, ("residual", 0))
            step("project_out", 0, ("store_attended", 0))
            step("residual", 0, ("project_out", 0))
    return needs


def plan_order():
    needs = step_needs()
    users = {step: [] for step in needs}
    for step, before in needs.items():
        for other in before:
            users[other].append(step)

    def cost(step):
        return ONE_HEAD_STEPS.get(step[0], STEPS.get(step[0])) if step[1] == MULTI else STEPS[step[0]]

    rest = {}

    def way(step):
        if step not in rest:
            rest[step] = (max(us + HANDOVER[e] for e, us in cost(step).items()) +
                          max([way(user) for user in users[step]], default=0.))
        return rest[step]

    def read_by(step):
        return ((READ_BY if step[1] < MULTI else READ_BY_ONE_HEAD)[step[0]],) + step[1:]

    free = dict.fromkeys(HANDOVER, 0.)
    done, starts, ring_w, ring_t = {}, {}, [], []
    attended_last, probs_of = None, {}
    while len(done) < len(needs):
        best = None
        for step in needs:
            kind, l, b, i = step
            if step in done or any(other not in done for other in needs[step]):
                continue
            awaited = list(needs[step])
            if kind in RING_W and len(ring_w) >= WORK:
                awaited.append(read_by(ring_w[-WORK]))
            if kind in RING_T and len(ring_t) >= SLOTS:
                awaited.append(read_by(ring_t[-SLOTS]))
            if l < MULTI:
                if kind == "attend" and attended_last:
                    awaited.append(("store_out", *attended_last[1:]))
                if kind == "exps" and i in probs_of:
                    awaited.append(("attend", *probs_of[i], i // PER))
                if kind == "scores_t" and i == 0 and ring_t and ring_t[-1][0] == kind and ring_t[-1][3] < HEADS - 1:
                    continue
            if any(other not in done for other in awaited):
                continue
            start = max([done[other] for other in awaited] + [free[e] for e in cost(step)], default=0.)
            rank = (start, -way(step) - LEAD * (b == 0) - FAVOURED.get(kind, 0.))
            if best is None or rank < best[0]:
                best = rank, step, start
        _, step, start = best
        kind, l, b, i = step
        starts[step] = start
        for e, us in cost(step).items():
            free[e] = start + us
        done[step] = max(start + us + HANDOVER[e] for e, us in cost(step).items())
        if kind in RING_W:
            ring_w.append(step)
        if kind in RING_T:
            ring_t.append(step)
        if kind == "attend" and l < MULTI:
            attended_last = step
        if kind == "exps" and l < MULTI:
            probs_of[i] = (l, b)
    return sorted(starts, key=starts.get)


ORDER = None


def attention_blocks(nc: bass.Bass, x, out, vectors, constants, weights):
    order = ORDER or plan_order()
    count, seen = {}, {}
    for kind, l, b, i in order:
        seen[kind] = seen.get(kind, 0) + 1
        count[kind, l, b, i] = seen[kind]

    def nth(kind, l, b, i=0):
        return count[kind, l, b, i]

    with ExitStack() as ctx:
        def sb(name, shape, dt=F32):
            return ctx.enter_context(nc.sbuf_tensor(name, shape, dt))

        def sem(name):
            return ctx.enter_context(nc.semaphore(name))

        xs = [sb(f"xs{b}", [C, T]) for b in range(B)]
        vec = sb("vec", [C, BLOCKS, NVEC])
        const = sb("const", [C, NCONST])
        w = [sb(f"w{l}", [C, 4, C]) for l in range(BLOCKS)]
        ident = const[:, 0:C]
        group_avg = const[:, C:2 * C]
        minus_half = const[:, HALF_COL:HALF_COL + 1]
        select = sb("select", [C, PAIRS, SELS, C], F32R)
        head_row = sb("head_row", [2, 2, C], F32R)

        bn = [sb(f"bn{b}", [C, 6]) for b in range(B)]
        mom = [sb(f"mom{b}", [C, 3]) for b in range(B)]
        grp = [sb(f"grp{b}", [C, 5]) for b in range(B)]
        hn = [sb(f"hn{b}", [C, T]) for b in range(B)]
        qk = [sb(f"qk{b}", [C, 2, T]) for b in range(B)]
        qk_high = [sb(f"qk_high{b}", [C, 2, T], F32R) for b in range(B)]
        qk_low = [sb(f"qk_low{b}", [C, 2, T], F32R) for b in range(B)]
        q_heads = [sb(f"q_heads{b}", [C, HEADS, T], F32R) for b in range(B)]
        k_pairs = [sb(f"k_pairs{b}", [C, PAIRS, T], F32R) for b in range(B)]
        v_heads = [sb(f"v_heads{b}", [C, NCH, HEADS, 2 * DH]) for b in range(B)]
        v_one = [sb(f"v_one{b}", [C, NCH, C]) for b in range(B)]
        neg_max = [sb(f"neg_max{b}", [C, PAIRS, NCH, 2]) for b in range(B)]
        neg_max_s = [sb(f"neg_max_s{b}", [C, NCH]) for b in range(B)]
        max_rows = [sb(f"max_rows{b}", [2, PAIRS, T], F32R) for b in range(B)]
        probs = sb("probs", [C, HEADS, NCH, T])
        p_one = [sb(f"p_one{b}", [C, NCH, T]) for b in range(B)]
        pt_one = [sb(f"pt_one{b}", [C, NCH, T]) for b in range(B)]
        sums = [sb(f"sums{b}", [C, NCH]) for b in range(B)]
        o_raw = [sb(f"o_raw{b}", [C, STACKS, T]) for b in range(B)]
        rden = [sb(f"rden{b}", [C, STACKS, PER * NCH]) for b in range(B)]
        o_tok = [sb(f"o_tok{b}", [C, NCH, C]) for b in range(B)]
        att = [sb(f"att{b}", [C, T]) for b in range(B)]

        def bank(name):
            return ctx.enter_context(nc.psum_tensor(name, [C, 512], F32))

        ps_w = [bank(f"ps_w{i}") for i in range(WORK)]
        ps_t = [bank(f"ps_t{i}") for i in range(SLOTS)]
        ps_m = [bank(f"ps_m{b}") for b in range(B)]
        ps_o = bank("ps_o")

        x_in = [sem(f"x_in{b}") for b in range(B)]
        const_in = sem("const_in")
        w_in = [sem(f"w_in{l}") for l in range(BLOCKS)]
        out_written = sem("out_written")
        zeros_ready = sem("zeros_ready")
        v_ones_ready = sem("v_ones_ready")
        vchain = sem("vchain")
        select_ready = sem("select_ready")
        head_row_ready = sem("head_row_ready")
        moments_done = sem("moments_done")
        means_done = sem("means_done")
        variance_ready, rsqrt_ready, h_ready = sem("variance_ready"), sem("rsqrt_ready"), sem("h_ready")
        qk_projected, v_projected = sem("qk_projected"), sem("v_projected")
        qk_rounded, v_stored, qk_split = sem("qk_rounded"), sem("v_stored"), sem("qk_split")
        q_placed, k_placed = sem("q_placed"), sem("k_placed")
        q_stored_even, q_stored_odd, k_stored = sem("q_stored_even"), sem("q_stored_odd"), sem("k_stored")
        scores_done, max_done = sem("scores_done"), sem("max_done")
        max_turned, max_stored = sem("max_turned"), sem("max_stored")
        scores_t_done, exps_done, attended = sem("scores_t_done"), sem("exps_done"), sem("attended")
        out_stored, out_turned, divided, out_back = (sem("out_stored"), sem("out_turned"), sem("divided"),
                                                     sem("out_back"))
        p_turned, p_stored = sem("p_turned"), sem("p_stored")
        att_stored, out_projected, x_ready = sem("att_stored"), sem("out_projected"), sem("x_ready")

        w_users = [s for s in order if s[0] in RING_W]
        w_slot = {s: n % WORK for n, s in enumerate(w_users)}
        t_users = [s for s in order if s[0] in RING_T]
        t_slot = {s: n % SLOTS for n, s in enumerate(t_users)}
        o_users = [s for s in order if s[0] == "attend" and s[1] < MULTI]

        block = ctx.enter_context(nc.Block())

        @block.sync
        def _(sp):
            sp.dma_start(xs[0][:, :], x[0]).then_inc(x_in[0], 16)
            sp.dma_start(const[:, :], constants).then_inc(const_in, 16)
            sp.dma_start(vec[:, :, :], vectors).then_inc(const_in, 16)
            sp.dma_start(w[0][:, :], weights[0]).then_inc(w_in[0], 16)
            sp.dma_start(xs[1][:, :], x[1]).then_inc(x_in[1], 16)
            for l in range(1, BLOCKS):
                sp.dma_start(w[l][:, :], weights[l]).then_inc(w_in[l], 16)
            for step in order:
                kind, l, b, i = step
                if kind == "write":
                    sp.wait_ge(x_ready, nth("residual", l, b))
                    sp.dma_start(out[b], xs[b][:, :]).then_inc(out_written, 16)
            sp.wait_ge(out_written, 16 * B)

        @block.gpsimd
        def _(pool):
            for b in range(B):
                nc.gpsimd.memset(q_heads[b][:, :, :].bitcast(F32), 0.0).then_inc(zeros_ready, 1)
                nc.gpsimd.memset(v_heads[b][:, :, :, :], 1.0).then_inc(v_ones_ready, 1)
            pool.wait_ge(const_in, 32)
            for pair in range(PAIRS):
                nc.gpsimd.tensor_scalar(select[:, pair, :, :].rearrange("p s c -> p (s c)"),
                                        const[:, SEL:SEL + SELS * C], const[:, PAIR_COL + pair:PAIR_COL + pair + 1],
                                        1.0, ALU.mult, ALU.mult).then_inc(select_ready, 1)
            for kind, l, b, i in order:
                if kind == "rsqrt":
                    pool.wait_ge(variance_ready, nth("variance", l, b))
                    nc.gpsimd.tensor_tensor(grp[b][:, 2:3], grp[b][:, 1:2], minus_half,
                                            ALU.pow).then_inc(rsqrt_ready, 1)

        @block.tensor
        def _(pe):
            mm = nc.tensor.matmul

            def ring_free(step):
                n = w_users.index(step)
                if n < WORK:
                    return
                kind, *which = w_users[n - WORK]
                l = which[0]
                if kind == "scores":
                    pe.wait_ge(max_done, nth("row_max", *which))
                elif kind == "place_q":
                    pe.wait_ge(q_stored_even, nth("store_q", *which))
                    pe.wait_ge(q_stored_odd, nth("store_q", *which))
                elif kind == "place_k":
                    pe.wait_ge(k_stored, nth("store_k", *which))
                elif l < MULTI:
                    pe.wait_ge(qk_split, nth("split", *which))
                else:
                    pe.wait_ge(qk_rounded, nth("round", *which))

            for step in order:
                kind, l, b, i = step
                multi = l < MULTI
                m = ps_m[b]
                if kind == "group_means":
                    if l == 0:
                        pe.wait_ge(const_in, 32)
                    pe.wait_ge(moments_done, nth("moments", l, b))
                    mm(m[:, 0:2], group_avg, mom[b][:, 0:3:2], start=True, stop=True).then_inc(means_done, 1)
                elif kind == "project":
                    if i == 0:
                        pe.wait_ge(w_in[l], 16)
                        pe.wait_ge(h_ready, nth("normalise", l, b))
                    ring_free(step)
                    mm(ps_w[w_slot[step]][:, 0:T], w[l][:, i, :], hn[b][:, :],
                       start=True, stop=True).then_inc(qk_projected, 1)
                elif kind == "project_v":
                    pe.wait_ge(w_in[l], 16)
                    pe.wait_ge(h_ready, nth("normalise", l, b))
                    for n in range(NCH):
                        last = mm(m[:, n * C:(n + 1) * C], hn[b][:, n * CHUNK:(n + 1) * CHUNK], w[l][:, 2, :],
                                  start=True, stop=True)
                    last.then_inc(v_projected, 1)
                elif kind in ("place_q", "place_k"):
                    k = int(kind == "place_k")
                    pe.wait_ge(qk_split, nth("split", l, b, k))
                    if l == 0:
                        pe.wait_ge(select_ready, (i + 1) * PAIRS // STACKS)
                    ring_free(step)
                    for n in range(2):
                        dst = ps_w[w_slot[step]][:, n * T:(n + 1) * T]
                        pair = 2 * i + n
                        mm(dst, select[:, pair, 2 * k, :], qk_high[b][:, k, :], start=True, stop=False)
                        last = mm(dst, select[:, pair, 2 * k + 1, :], qk_low[b][:, k, :], start=False, stop=True)
                    last.then_inc(k_placed if k else q_placed, 1)
                elif kind == "scores":
                    if multi and i % PER == 0:
                        pe.wait_ge(q_stored_even, nth("store_q", l, b, i // PER))
                        pe.wait_ge(q_stored_odd, nth("store_q", l, b, i // PER))
                        pe.wait_ge(k_stored, nth("store_k", l, b, i // PER))
                    elif not multi:
                        pe.wait_ge(qk_rounded, nth("round", l, b, 1))
                    ring_free(step)
                    for qc in range(NCH):
                        cols = slice(qc * CHUNK, (qc + 1) * CHUNK)
                        lhs = q_heads[b][:, i, cols] if multi else qk[b][:, 0, cols]
                        rhs = k_pairs[b][:, i // 2, :] if multi else qk[b][:, 1, :]
                        last = mm(ps_w[w_slot[step]][:, qc * T:(qc + 1) * T], lhs, rhs, start=True, stop=True)
                    last.then_inc(scores_done, 1)
                elif kind == "turn_max":
                    pe.wait_ge(max_done, nth("row_max", l, b, 2 * i + 1))
                    if i == 0:
                        pe.wait_ge(v_stored, nth("store_v", l, b))
                    else:
                        pe.wait_ge(max_stored, nth("store_max", l, b, i - 1))
                    for qc in range(NCH):
                        last = nc.tensor.transpose(m[0:2, qc * CHUNK:(qc + 1) * CHUNK], neg_max[b][:, i, qc, :],
                                                   ident)
                    last.then_inc(max_turned, 1)
                elif kind == "scores_t":
                    pair = i // 2
                    if i % 2 == 0:
                        pe.wait_ge(max_stored, nth("store_max", l, b, pair))
                    if l == 0 and i == 0:
                        pe.wait_ge(head_row_ready, 1)
                    n = t_users.index(step)
                    if n >= SLOTS:
                        pe.wait_ge(exps_done, nth("exps", *t_users[n - SLOTS][1:]))
                    for kc in range(NCH):
                        dst = ps_t[t_slot[step]][:, kc * T:(kc + 1) * T]
                        keys = slice(kc * CHUNK, (kc + 1) * CHUNK)
                        mm(dst, k_pairs[b][:, pair, keys], q_heads[b][:, i, :], start=True, stop=False)
                        last = mm(dst, head_row[:, i % 2, :], max_rows[b][:, pair, :], start=False, stop=True)
                    last.then_inc(scores_t_done, 1)
                elif kind == "attend" and multi:
                    pe.wait_ge(exps_done, nth("exps", l, b, PER * (i + 1) - 1))
                    if l == 0 and i == 0:
                        pe.wait_ge(v_ones_ready, b + 1)
                    pe.wait_ge(v_stored, nth("store_v", l, b))
                    n = o_users.index(step)
                    if n > 0:
                        pe.wait_ge(out_stored, nth("store_out", *o_users[n - 1][1:]))
                    for kc in range(NCH):
                        for j in range(PER):
                            h = PER * i + j
                            last = mm(ps_o[QUAD * j:QUAD * (j + 1), i * T:(i + 1) * T], v_heads[b][:, kc, h, :],
                                      probs[:, h, kc, :], start=(kc == 0), stop=(kc == NCH - 1))
                    last.then_inc(attended, 1)
                elif kind == "attend":
                    pe.wait_ge(p_stored, nth("store_p", l, b))
                    pe.wait_ge(v_stored, nth("store_v", l, b))
                    for kc in range(NCH):
                        last = mm(m[:, 0:T], v_one[b][:, kc, :], pt_one[b][:, kc, :],
                                  start=(kc == 0), stop=(kc == NCH - 1))
                    last.then_inc(attended, 1)
                elif kind == "turn_p":
                    pe.wait_ge(divided, nth("divide", l, b))
                    n = t_users.index(step)
                    prev = t_users[n - SLOTS]
                    if prev[0] == "scores_t":
                        pe.wait_ge(exps_done, nth("exps", *prev[1:]))
                    else:
                        pe.wait_ge(p_stored, nth("store_p", *prev[1:3]))
                    for kc in range(NCH):
                        for qc in range(NCH):
                            at = kc * T + qc * CHUNK
                            last = nc.tensor.transpose(ps_t[t_slot[step]][:, at:at + CHUNK],
                                                       p_one[b][:, qc, kc * CHUNK:(kc + 1) * CHUNK], ident)
                    last.then_inc(p_turned, 1)
                elif kind == "turn_out":
                    pe.wait_ge(out_stored, nth("store_out", l, b, i))
                    if i == 0:
                        pe.wait_ge(max_stored, nth("store_max", l, b, PAIRS - 1))
                    else:
                        pe.wait_ge(divided, nth("divide", l, b, i - 1))
                    for qc in range(NCH):
                        at = (i * NCH + qc) * C
                        last = nc.tensor.transpose(m[:, at:at + C], o_raw[b][:, i, qc * CHUNK:(qc + 1) * CHUNK],
                                                   ident)
                    last.then_inc(out_turned, 1)
                elif kind == "turn_back":
                    pe.wait_ge(divided, nth("divide", l, b, STACKS - 1))
                    for qc in range(NCH):
                        last = nc.tensor.transpose(m[:, qc * CHUNK:(qc + 1) * CHUNK], o_tok[b][:, qc, :], ident)
                    last.then_inc(out_back, 1)
                elif kind == "project_out":
                    pe.wait_ge(att_stored, nth("store_attended", l, b))
                    mm(m[:, 0:T], w[l][:, 3, :], att[b][:, :], start=True, stop=True).then_inc(out_projected, 1)

        @block.scalar
        def _(act):
            act.wait_ge(const_in, 32)
            for step in order:
                kind, l, b, i = step
                multi = l < MULTI
                m = ps_m[b]
                if kind == "round":
                    act.wait_ge(qk_projected, nth("project", l, b, i))
                    dst = (qk_high if multi else qk)[b][:, i, :]
                    nc.scalar.activation(dst, ps_w[w_slot["project", l, b, i]][:, 0:T], ACT.Identity,
                                         bias=vec[:, l, BQ + i:BQ + i + 1]).then_inc(qk_rounded, 1)
                elif kind == "store_q":
                    act.wait_ge(q_placed, nth("place_q", l, b, i))
                    if l == 0:
                        act.wait_ge(zeros_ready, b + 1)
                    src = ps_w[w_slot["place_q", l, b, i]][0:HALF, :].rearrange("p (n t) -> p n t", n=2)
                    nc.scalar.activation(q_heads[b][0:HALF, PER * i:PER * (i + 1):2, :], src,
                                         ACT.Copy).then_inc(q_stored_even, 1)
                elif kind == "store_k":
                    act.wait_ge(k_placed, nth("place_k", l, b, i))
                    dst = k_pairs[b][:, 2 * i:2 * i + 2, :].rearrange("p n t -> p (n t)")
                    nc.scalar.activation(dst, ps_w[w_slot["place_k", l, b, i]][:, :], ACT.Copy).then_inc(k_stored, 1)
                elif kind == "store_v":
                    act.wait_ge(v_projected, nth("project_v", l, b))
                    if multi:
                        if l == 0:
                            act.wait_ge(v_ones_ready, b + 1)
                        dst = v_heads[b][:, :, :, 0:DH].rearrange("p c h d -> p (c h) d")
                        src = m[:, 0:NCH * C].rearrange("p (c d) -> p c d", d=DH)
                    else:
                        dst = v_one[b][:, :, :].rearrange("p c d -> p (c d)")
                        src = m[:, 0:NCH * C]
                    nc.scalar.activation(dst, src, ACT.Copy).then_inc(v_stored, 1)
                elif kind == "store_max":
                    act.wait_ge(max_turned, nth("turn_max", l, b, i))
                    nc.scalar.activation(max_rows[b][:, i, :], m[0:2, 0:T],
                                         ACT.Copy).then_inc(max_stored, 1)
                elif kind == "exps" and multi:
                    act.wait_ge(scores_t_done, nth("scores_t", l, b, i))
                    if i % PER == 0:
                        users = [s for s in order[:order.index(step)] if s[0] == "attend" and s[3] == i // PER]
                        if users:
                            act.wait_ge(attended, nth(*users[-1]))
                    src = ps_t[t_slot["scores_t", l, b, i]][:, :]
                    nc.scalar.activation(probs[:, i, :, :].rearrange("p c t -> p (c t)"), src, ACT.Exp,
                                         scale=SCALE).then_inc(exps_done, 1)
                elif kind == "exps":
                    act.wait_ge(max_done, nth("row_max", l, b, 0))
                    for qc in range(NCH):
                        src = ps_w[w_slot["scores", l, b, 0]][:, qc * T:(qc + 1) * T]
                        last = nc.scalar.activation(p_one[b][:, qc, :], src, ACT.Exp, scale=SCALE_ONE,
                                                    bias=neg_max_s[b][:, qc:qc + 1],
                                                    accum_out=sums[b][:, qc:qc + 1])
                    last.then_inc(exps_done, 1)
                elif kind == "store_p":
                    act.wait_ge(p_turned, nth("turn_p", l, b))
                    nc.scalar.activation(pt_one[b][:, :, :].rearrange("p c t -> p (c t)"),
                                         ps_t[t_slot["turn_p", l, b, 0]][:, :], ACT.Copy).then_inc(p_stored, 1)
                elif kind == "store_out":
                    act.wait_ge(attended, nth("attend", l, b, i))
                    nc.scalar.activation(o_raw[b][:, i, :], ps_o[:, i * T:(i + 1) * T],
                                         ACT.Copy).then_inc(out_stored, 1)
                elif kind == "store_attended":
                    if multi:
                        act.wait_ge(out_back, nth("turn_back", l, b))
                    else:
                        act.wait_ge(attended, nth("attend", l, b, 0))
                    nc.scalar.activation(att[b][:, :], m[:, 0:T], ACT.Identity,
                                         bias=vec[:, l, BV:BV + 1]).then_inc(att_stored, 1)

        @block.vector
        def _(dve):
            links = [0]

            def link(ins):
                links[0] += 1
                ins.then_inc(vchain, 1)
                dve.wait_ge(vchain, links[0])

            tt, ts, stt = nc.vector.tensor_tensor, nc.vector.tensor_scalar, nc.vector.scalar_tensor_tensor
            for step in order:
                kind, l, b, i = step
                multi = l < MULTI
                m = ps_m[b]
                if kind == "moments":
                    if l == 0:
                        dve.wait_ge(x_in[b], 16)
                    else:
                        dve.wait_ge(x_ready, nth("residual", l - 1, b))
                    link(nc.vector.bn_stats(bn[b][:, :], xs[b][:, :]))
                    link(nc.vector.bn_aggr(mom[b][:, 0:2], bn[b][:, :]))
                    stt(out=mom[b][:, 2:3], in0=mom[b][:, 0:1], scalar=mom[b][:, 0:1], in1=mom[b][:, 1:2],
                        op0=ALU.mult, op1=ALU.add).then_inc(moments_done, 1)
                elif kind == "variance":
                    g = grp[b]
                    if l == 0:
                        dve.wait_ge(const_in, 32)
                        if b == 0:
                            nc.vector.tensor_copy(head_row[:, :, :].rearrange("p j c -> p (j c)"),
                                                  const[0:2, ROWS:ROWS + 2 * C]).then_inc(head_row_ready, 1)
                    dve.wait_ge(means_done, nth("group_means", l, b))
                    link(ts(g[:, 0:1], m[:, 0:1], m[:, 0:1], m[:, 1:2], ALU.mult, ALU.subtract))
                    ts(g[:, 1:2], g[:, 0:1], -1.0, EPS[l], ALU.mult, ALU.add).then_inc(variance_ready, 1)
                elif kind == "normalise":
                    g = grp[b]
                    dve.wait_ge(rsqrt_ready, nth("rsqrt", l, b))
                    link(ts(g[:, 3:4], g[:, 2:3], vec[:, l, GN_W:GN_W + 1], None, ALU.mult))
                    link(ts(g[:, 4:5], m[:, 0:1], g[:, 3:4], vec[:, l, GN_B:GN_B + 1], ALU.mult, ALU.subtract))
                    ts(hn[b][:, :], xs[b][:, :], g[:, 3:4], g[:, 4:5], ALU.mult, ALU.subtract).then_inc(h_ready, 1)
                elif kind == "split":
                    dve.wait_ge(qk_rounded, nth("round", l, b, i))
                    stt(out=qk_low[b][:, i, :], in0=ps_w[w_slot["project", l, b, i]][:, 0:T],
                        scalar=vec[:, l, BQ + i:BQ + i + 1], in1=qk_high[b][:, i, :].bitcast(F32),
                        op0=ALU.add, op1=ALU.subtract).then_inc(qk_split, 1)
                elif kind == "store_q":
                    dve.wait_ge(q_placed, nth("place_q", l, b, i))
                    if l == 0:
                        dve.wait_ge(zeros_ready, b + 1)
                    src = ps_w[w_slot["place_q", l, b, i]][HALF:C, :].rearrange("p (n t) -> p n t", n=2)
                    nc.vector.tensor_copy(q_heads[b][HALF:C, PER * i + 1:PER * (i + 1):2, :],
                                          src).then_inc(q_stored_odd, 1)
                elif kind == "row_max":
                    dve.wait_ge(scores_done, nth("scores", l, b, i))
                    src = ps_w[w_slot["scores", l, b, i]][:, :].rearrange("p (c t) -> p c t", c=NCH)
                    red = nc.vector.tensor_reduce(neg_max[b][:, i // 2, :, i % 2], src, AX_X, ALU.max,
                                                  negate=True)
                    if multi:
                        red.then_inc(max_done, 1)
                    else:
                        link(red)
                        ts(neg_max_s[b][:, :], neg_max[b][:, 0, :, 0], SCALE_ONE, None, ALU.mult).then_inc(max_done, 1)
                elif kind == "divide" and multi:
                    dve.wait_ge(out_turned, nth("turn_out", l, b, i))
                    src = m[:, i * NCH * C:(i + 1) * NCH * C].rearrange("p (n e) -> p n e", e=2 * DH)
                    link(nc.vector.reciprocal(rden[b][:, i, :], src[:, :, DH:DH + 1].rearrange("p n e -> p (n e)")))
                    src = m[:, i * NCH * C:(i + 1) * NCH * C].rearrange("p (c j e) -> p c j e", c=NCH, e=2 * DH)
                    dst = o_tok[b][:, :, i * HALF:(i + 1) * HALF].rearrange("p c (j d) -> p c j d", d=DH)
                    by = rden[b][:, i, :].rearrange("p (c j) -> p c j", c=NCH).unsqueeze(3)
                    tt(dst, src[:, :, :, 0:DH], by.to_broadcast([C, NCH, PER, DH]), ALU.mult).then_inc(divided, 1)
                elif kind == "divide":
                    dve.wait_ge(exps_done, nth("exps", l, b, 0))
                    link(nc.vector.reciprocal(rden[b][:, 0, 0:NCH], sums[b][:, :]))
                    for qc in range(NCH):
                        last = ts(p_one[b][:, qc, :], p_one[b][:, qc, :], rden[b][:, 0, qc:qc + 1], None, ALU.mult)
                    last.then_inc(divided, 1)
                elif kind == "residual":
                    dve.wait_ge(out_projected, nth("project_out", l, b))
                    stt(out=xs[b][:, :], in0=m[:, 0:T], scalar=vec[:, l, BP:BP + 1], in1=xs[b][:, :],
                        op0=ALU.add, op1=ALU.add).then_inc(x_ready, 1)


def kernel(**inputs):
    import numpy as np
    import concourse.bacc as bacc
    from concourse.bass_utils import run_bass_kernel_spmd

    a = {k: np.asarray(v) for k, v in inputs.items()}
    wq, wk, wv, wp = {}, {}, {}, {}
    bq, bk, bv, bp, gw, gb = {}, {}, {}, {}, {}, {}
    p = "L0_conv_"
    wq[0], wk[0], wv[0], wp[0] = (a[p + n] for n in ("wq", "wk", "wv", "wp"))
    bq[0], bk[0], bv[0], bp[0] = (a[p + n] for n in ("bq", "bk", "bv", "bp"))
    gw[0], gb[0] = a[p + "gn_w"], a[p + "gn_b"]
    p = "L1_conv_"
    wq[1], wk[1], wv[1] = (a[p + "w1"][n * C:(n + 1) * C] for n in range(3))
    bq[1], bk[1], bv[1] = (a[p + "b1"][n * C:(n + 1) * C] for n in range(3))
    wp[1], bp[1], gw[1], gb[1] = a[p + "w2"], a[p + "b2"], a[p + "gn_w"], a[p + "gn_b"]
    p = "L2_conv_"
    wq[2], bq[2], wp[2], bp[2] = a[p + "wq"], a[p + "bq"], a[p + "wproj"], a[p + "bproj"]
    wk[2], wv[2] = (a[p + "wkv"][n * C:(n + 1) * C] for n in range(2))
    bk[2], bv[2] = (a[p + "bkv"][n * C:(n + 1) * C] for n in range(2))
    gw[2], gb[2] = a[p + "gn_weight"], a[p + "gn_bias"]
    p = "L3_conv_"
    wq[3], wk[3], wv[3] = (a[p + "qkv_w"][n * C:(n + 1) * C] for n in range(3))
    bq[3], bk[3], bv[3] = (a[p + "qkv_b"][n * C:(n + 1) * C] for n in range(3))
    wp[3], bp[3], gw[3], gb[3] = a[p + "proj_w"], a[p + "proj_b"], a[p + "gn_scale"], a[p + "gn_bias"]

    vectors = np.zeros((C, BLOCKS, NVEC), np.float32)
    arrays = {"x": np.ascontiguousarray(a["x"].reshape(B, C, T))}
    for l in range(BLOCKS):
        arrays[f"w{l}"] = np.ascontiguousarray(np.stack([wq[l].T, wk[l].T, wv[l].T, wp[l].T], axis=1))
        for at, v in ((GN_W, gw), (GN_B, gb), (BQ, bq), (BK, bk), (BV, bv), (BP, bp)):
            vectors[:, l, at] = v[l]
    arrays["vectors"] = vectors
    constants = np.zeros((C, NCONST), np.float32)
    constants[:, 0:C] = np.eye(C)
    constants[:, C:2 * C] = np.kron(np.eye(C // GROUP), np.full((GROUP, GROUP), 1.0 / GROUP))
    one, none = np.eye(DH), np.zeros((DH, DH))
    for n, blocks in enumerate(([one, none, one, none], [none, one, none, none],
                                [one, one, none, none], [none, none, one, none])):
        of_pair = np.kron(np.eye(2), np.concatenate(blocks, axis=1))
        constants[:, SEL + n * C:SEL + (n + 1) * C] = np.tile(of_pair, (PAIRS, 1))
    constants[:, PAIR_COL:PAIR_COL + PAIRS] = np.kron(np.eye(PAIRS), np.ones((C // PAIRS, 1)))
    constants[0:2, ROWS:ROWS + 2 * C] = np.kron(np.eye(2), np.ones((1, C)))
    constants[:, HALF_COL] = -0.5
    arrays["constants"] = constants

    nc = bacc.Bacc("TRN2", target_bir_lowering=False, num_devices=1)
    ap = {n: nc.dram_tensor(f"in_{n}", v.shape, mybir.dt.float32, kind="ExternalInput").ap() for n, v in arrays.items()}
    out = nc.dram_tensor("out", (B, C, T), mybir.dt.float32, kind="ExternalOutput").ap()
    attention_blocks(nc, ap["x"], out, ap["vectors"], ap["constants"], [ap[f"w{l}"] for l in range(BLOCKS)])
    r = run_bass_kernel_spmd(nc, [{f"in_{n}": v for n, v in arrays.items()}], core_ids=[0])
    return r.results[0]["out"].reshape(a["x"].shape)
```

```python
from contextlib import ExitStack

import concourse.bass as bass
from concourse import mybir

F32 = mybir.dt.float32
F32R = mybir.dt.float32r
ACT = mybir.ActivationFunctionType
ALU = mybir.AluOpType
AX_X = mybir.AxisListType.X

B, C, T = 2, 128, 256
HEADS, DH = 8, 16
STACKS, PER = 2, 4
QUAD = 32
PAIRS = HEADS // 2
HALF = C // 2
MAX_ROW = 2 * DH
MULTI = 3
BLOCKS = 4
CHUNK = 128
NCH = T // CHUNK
GROUP = 4
EPS = [1e-5, 1e-5, 1e-5, 1e-6]
SCALE = DH ** -0.5
SCALE_ONE = C ** -0.5
WORK, SLOTS = 3, 2

GN_W, GN_B, BQ, BK, BV, BP = range(6)
NVEC = 6
SELS = 4
PAIR_COL = 2 * C
ONES_COL = PAIR_COL + PAIRS
HALF_COL = ONES_COL + 1
EPS_COL = HALF_COL + 1
NCONST = EPS_COL + 3 * BLOCKS

STEPS = {
    "scale_w": {"A": .6}, "select": {"A": .5}, "fold_bias": {"P": .3}, "add_bias": {"V": .07},
    "moments": {"V": .8}, "group_means": {"P": .15}, "variance": {"V": .19}, "rsqrt": {"G": .5},
    "normalise": {"V": .33}, "project": {"P": .43}, "round": {"A": .36}, "split": {"V": .4},
    "project_v": {"P": .43}, "store_v": {"V": .33}, "place_q": {"P": .44}, "place_k": {"P": .44},
    "store_q": {"A": .48, "V": .6}, "store_k": {"A": .57}, "scores": {"P": .22}, "row_max": {"V": .6},
    "turn_max": {"P": .22}, "store_max": {"A": .52}, "scores_t": {"P": .22}, "exps": {"A": .48},
    "attend": {"P": 1.01}, "store_out": {"A": .27}, "turn_out": {"P": .22}, "divide": {"V": .44},
    "turn_back": {"P": .22}, "store_attended": {"V": .35}, "project_out": {"P": .43}, "residual": {"V": .4},
}
ONE_HEAD_STEPS = {
    "scores": {"P": .43}, "row_max": {"V": .3}, "exps": {"A": .45}, "divide": {"V": .5}, "turn_p": {"P": .22},
    "store_p": {"A": .27}, "scale_q": {"V": .4}, "attend": {"P": .43}, "store_attended": {"V": .22},
    "project_out": {"P": .22}, "residual": {"V": .22}, "write": {"S": .1},
}
HANDOVER = {"P": .2, "A": .3, "V": .2, "G": .1, "S": 2.}
READ_BY = {"project": "split", "place_q": "store_q", "place_k": "store_k", "scores": "row_max",
           "scores_t": "exps", "turn_p": "store_p", "fold_bias": "add_bias"}
READ_BY_ONE_HEAD = {"fold_bias": "add_bias", "project": "round", "scores": "exps", "turn_p": "store_p",
                    "attend": "store_attended", "project_out": "residual"}


def ring_of(step):
    kind, l = step[:2]
    if kind in ("fold_bias", "project", "place_q", "place_k", "scores"):
        return "w"
    if kind in ("attend", "project_out") and l == MULTI:
        return "w"
    if kind in ("scores_t", "turn_p"):
        return "t"
    return None


def read_by(step):
    if step[0] == "project" and step[1] == MULTI and step[3] == 0:
        return ("scale_q",) + step[1:]
    return ((READ_BY if step[1] < MULTI else READ_BY_ONE_HEAD)[step[0]],) + step[1:]


LANDED = {("moments", 0, 0, 0): 3., ("scale_w", 0, 0, 0): 4.5, ("group_means", 0, 0, 0): 4.5,
          ("variance", 0, 0, 0): 5.4, ("fold_bias", 0, 0, 0): 6.6, ("moments", 0, 1, 0): 5.8}
WARM_COST = .22
LONG_GAP = 1.5
SLOW_UNTIL = 6.
LEAD = [24, 13, -69, -26]
FAVOURED = {"exps": -10, "row_max": -5, "store_k": -10, "store_max": 10, "turn_max": 10}


def cost(step):
    return ONE_HEAD_STEPS.get(step[0], STEPS.get(step[0])) if step[1] == MULTI else STEPS[step[0]]


def in_turn(other, step):
    return other[0] == step[0] or list(cost(other)) == list(cost(step)) == ["P"]


def step_needs():
    needs = {}
    for b in range(B):
        for l in range(BLOCKS):
            def step(kind, i, *others):
                needs[kind, l, b, i] = [(k, l, b, j) for k, j in others]

            if b == 0:
                needs["scale_w", l, 0, 0] = needs["fold_bias", l, 0, 0] = [("project_v", l - 1, 1, 0)] * min(l, 1)
                step("add_bias", 0, ("fold_bias", 0))
            if b == l == 0:
                for n in range(PAIRS):
                    step("select", n, ("select", n - 1) if n else ("scale_w", 0))
            step("moments", 0)
            if l > 0:
                needs["moments", l, b, 0] = [("residual", l - 1, b, 0)]
            step("group_means", 0, ("moments", 0))
            step("variance", 0, ("group_means", 0))
            step("rsqrt", 0, ("variance", 0))
            step("normalise", 0, ("rsqrt", 0))
            for n in range(2):
                step("project", n, ("normalise", 0), *[("project", 0)] * n)
                needs["project", l, b, n].append(("scale_w", l, 0, 0))
                stored = "scale_q" if l == MULTI and n == 0 else "round"
                step(stored, n, ("project", n))
                needs[stored, l, b, n].append(("add_bias", l, 0, 0))
                if l < MULTI:
                    step("split", n, ("round", n))
            step("project_v", 0, ("normalise", 0))
            needs["project_v", l, b, 0].append(("scale_w", l, 0, 0))
            step("store_v", 0, ("project_v", 0))
            if l < MULTI:
                for n in range(STACKS):
                    step("place_q", n, ("split", 0), *[("place_k", n - 1)] * n)
                    needs["place_q", l, b, n].append(("select", 0, 0, 2 * n + 1))
                    step("place_k", n, ("split", 1), ("place_q", n))
                    step("store_q", n, ("place_q", n))
                    step("store_k", n, ("place_k", n))
                    step("attend", n, ("store_v", 0), *[("exps", PER * n + j) for j in range(PER)],
                         *[("store_out", n - 1)] * n)
                    step("store_out", n, ("attend", n))
                    step("turn_out", n, ("store_out", n), ("store_max", PAIRS - 1), *[("divide", n - 1)] * n)
                    step("divide", n, ("turn_out", n))
                for n in range(PAIRS):
                    step("turn_max", n, ("store_v", 0), ("row_max", 2 * n), ("row_max", 2 * n + 1),
                         *[("store_max", n - 1)] * min(n, 1))
                    step("store_max", n, ("turn_max", n))
                for h in range(HEADS):
                    after = [("scores", h - 1), ("row_max", h - 1), ("scores_t", h - 1), ("exps", h - 1)] * min(h, 1)
                    step("scores", h, ("store_q", h // PER), ("store_k", h // PER), *after[0:1])
                    step("row_max", h, ("scores", h), *after[1:2])
                    step("scores_t", h, ("store_max", h // 2), *after[2:3])
                    step("exps", h, ("scores_t", h), *after[3:4])
                step("turn_back", 0, ("divide", STACKS - 1))
                step("store_attended", 0, ("turn_back", 0))
            else:
                for qc in range(NCH):
                    chain = ["scores", "row_max", "exps", "divide", "turn_p", "store_p", "attend", "store_attended",
                             "project_out", "residual", "write"]
                    for kind, before in zip(chain, ["round"] + chain):
                        step(kind, qc, (before, 1 if before == "round" else qc))
                    needs["scores", l, b, qc].append(("scale_q", l, b, 0))
                    needs["attend", l, b, qc].append(("store_v", l, b, 0))
                continue
            step("project_out", 0, ("store_attended", 0))
            step("residual", 0, ("project_out", 0))
    return needs


def plan_order():
    needs = step_needs()
    users = {step: [] for step in needs}
    for step, before in needs.items():
        for other in before:
            users[other].append(step)

    rest = {}

    def way(step):
        if step not in rest:
            rest[step] = (max(us + HANDOVER[e] for e, us in cost(step).items()) +
                          max([way(user) for user in users[step]], default=0.))
        return rest[step]

    free = dict.fromkeys(HANDOVER, 0.)
    landed = LANDED
    done, starts, ring_w, ring_t = {}, {}, [], []
    attended_last, probs_of = None, {}
    while len(done) < len(needs):
        best = None
        for step in needs:
            kind, l, b, i = step
            if step in done or any(other not in done for other in needs[step]):
                continue
            awaited = list(needs[step])
            if ring_of(step) == "w" and len(ring_w) >= WORK:
                awaited.append(read_by(ring_w[-WORK]))
            if ring_of(step) == "t" and len(ring_t) >= SLOTS:
                awaited.append(read_by(ring_t[-SLOTS]))
            if l < MULTI:
                if kind == "attend" and attended_last:
                    awaited.append(("store_out", *attended_last[1:]))
                if kind == "exps" and i in probs_of:
                    awaited.append(("attend", *probs_of[i], i // PER))
                if kind == "scores_t" and i == 0 and ring_t and ring_t[-1][0] == kind and ring_t[-1][3] < HEADS - 1:
                    continue
            if any(other not in done for other in awaited):
                continue
            start = max([done[other] - (HANDOVER[next(iter(cost(other)))] if in_turn(other, step) else 0.)
                         for other in awaited] + [free[e] for e in cost(step)] + [landed.get(step, 0.)])
            rank = (start, -way(step) - LEAD[l] * (b == 0) - FAVOURED.get(kind, 0.))
            if best is None or rank < best[0]:
                best = rank, step, start
        _, step, start = best
        kind, l, b, i = step
        starts[step] = start
        for e, us in cost(step).items():
            free[e] = start + us
        done[step] = max(start + us + HANDOVER[e] for e, us in cost(step).items())
        if ring_of(step) == "w":
            ring_w.append(step)
        if ring_of(step) == "t":
            ring_t.append(step)
        if kind == "attend" and l < MULTI:
            attended_last = step
        if kind == "exps" and l < MULTI:
            probs_of[i] = (l, b)
    gap_from, bank_from, warm = 0., 1., 0
    for step in sorted(starts, key=starts.get):
        kind, l, b, i = step
        if "P" not in cost(step):
            continue
        t = max(gap_from, bank_from)
        fill = starts[step] - gap_from > LONG_GAP or gap_from < SLOW_UNTIL
        while fill and t + WARM_COST * (t >= SLOW_UNTIL) < starts[step]:
            starts["warm", 0, 0, warm] = t
            warm += 1
            t += WARM_COST * (1 + (t < SLOW_UNTIL))
        gap_from = starts[step] + cost(step)["P"]
        if kind == "attend" and l < MULTI:
            bank_from = done["store_out", l, b, i]
    return sorted(starts, key=starts.get)




def attention_blocks(nc: bass.Bass, x, out, vectors, constants, row_selections, weights):
    order = plan_order()
    count, seen = {}, {}
    for kind, l, b, i in order:
        seen[kind] = seen.get(kind, 0) + 1
        count[kind, l, b, i] = seen[kind]

    def nth(kind, l, b, i=0):
        return count[kind, l, b, i]

    with ExitStack() as ctx:
        def sb(name, shape, dt=F32):
            return ctx.enter_context(nc.sbuf_tensor(name, shape, dt))

        def sem(name):
            return ctx.enter_context(nc.semaphore(name))

        xs = [sb(f"xs{b}", [C, T]) for b in range(B)]
        vec = sb("vec", [C, BLOCKS, NVEC])
        const = sb("const", [C, NCONST])
        w = [sb(f"w{l}", [C, 4, C]) for l in range(BLOCKS)]
        ws = [sb(f"ws{l}", [C, 3, C]) for l in range(BLOCKS)]
        bias = sb("bias", [C, BLOCKS, 3])
        ident = const[:, 0:C]
        group_avg = const[:, C:2 * C]
        ones_rows = const[:, ONES_COL:ONES_COL + 1]
        minus_half = const[:, HALF_COL:HALF_COL + 1]
        selections = sb("selections", [C, SELS * C])
        blank, blank_exp = sb("blank", [C, C]), sb("blank_exp", [C, 1])
        select = sb("select", [C, PAIRS, SELS, C], F32R)

        bn = [sb(f"bn{b}", [C, 6]) for b in range(B)]
        mom = [sb(f"mom{b}", [C, 5]) for b in range(B)]
        grp = [sb(f"grp{b}", [C, 2]) for b in range(B)]
        hn = [sb(f"hn{b}", [C, T]) for b in range(B)]
        qk = [sb(f"qk{b}", [C, 2, T]) for b in range(B)]
        qk_high = [sb(f"qk_high{b}", [C, 2, T], F32R) for b in range(B)]
        qk_low = [sb(f"qk_low{b}", [C, 2, T], F32R) for b in range(B)]
        q_heads = [sb(f"q_heads{b}", [C, HEADS, T], F32R) for b in range(B)]
        k_pairs = [sb(f"k_pairs{b}", [C, PAIRS, T], F32R) for b in range(B)]
        v_heads = [sb(f"v_heads{b}", [C, NCH, HEADS, 2 * DH]) for b in range(B)]
        v_one = [sb(f"v_one{b}", [C, NCH, C]) for b in range(B)]
        neg_max = [sb(f"neg_max{b}", [C, PAIRS, NCH, QUAD + 1]) for b in range(B)]
        neg_max_one = [sb(f"neg_max_one{b}", [C, NCH]) for b in range(B)]
        probs = sb("probs", [C, HEADS, NCH, T])
        p_one = [sb(f"p_one{b}", [C, NCH, T]) for b in range(B)]
        pt_one = [sb(f"pt_one{b}", [C, NCH, T]) for b in range(B)]
        sums = [sb(f"sums{b}", [C, NCH]) for b in range(B)]
        o_raw = [sb(f"o_raw{b}", [C, STACKS, T]) for b in range(B)]
        rden = [sb(f"rden{b}", [C, STACKS, PER * NCH]) for b in range(B)]
        o_tok = [sb(f"o_tok{b}", [C, NCH, C]) for b in range(B)]
        att = [sb(f"att{b}", [C, T]) for b in range(B)]

        def bank(name):
            return ctx.enter_context(nc.psum_tensor(name, [C, 512], F32))

        ps_w = [bank(f"ps_w{i}") for i in range(WORK)]
        ps_t = [bank(f"ps_t{i}") for i in range(SLOTS)]
        ps_m = [bank(f"ps_m{b}") for b in range(B)]
        ps_o = bank("ps_o")

        x_in = [sem(f"x_in{b}") for b in range(B)]
        const_in, vec_in = sem("const_in"), sem("vec_in")
        w_in = [sem(f"w_in{l}") for l in range(BLOCKS)]
        out_written = sem("out_written")
        zeros_ready = [sem(f"zeros_ready{b}") for b in range(B)]
        max_zeros_ready = sem("max_zeros_ready")
        v_ones_ready = sem("v_ones_ready")
        vchain = sem("vchain")
        selections_in, select_ready = sem("selections_in"), sem("select_ready")
        warm_ready = sem("warm_ready")
        w_scaled, bias_folded, bias_ready = sem("w_scaled"), sem("bias_folded"), sem("bias_ready")
        moments_done = sem("moments_done")
        means_done = sem("means_done")
        variance_ready, rsqrt_ready, h_ready = sem("variance_ready"), sem("rsqrt_ready"), sem("h_ready")
        qk_projected, v_projected = sem("qk_projected"), sem("v_projected")
        qk_rounded, v_stored, qk_split = sem("qk_rounded"), sem("v_stored"), sem("qk_split")
        q_placed, k_placed = sem("q_placed"), sem("k_placed")
        q_stored_even, q_stored_odd, k_stored = sem("q_stored_even"), sem("q_stored_odd"), sem("k_stored")
        scores_done, max_done = sem("scores_done"), sem("max_done")
        max_turned = sem("max_turned")
        max_stored = sem("max_stored")
        scores_t_done, exps_done, attended = sem("scores_t_done"), sem("exps_done"), sem("attended")
        out_stored, out_turned, divided, out_back = (sem("out_stored"), sem("out_turned"), sem("divided"),
                                                     sem("out_back"))
        q_scaled = sem("q_scaled")
        p_turned, p_stored = sem("p_turned"), sem("p_stored")
        att_stored, out_projected, x_ready = sem("att_stored"), sem("out_projected"), sem("x_ready")

        w_users = [s for s in order if ring_of(s) == "w"]
        w_slot = {s: n % WORK for n, s in enumerate(w_users)}
        t_users = [s for s in order if ring_of(s) == "t"]
        t_slot = {s: n % SLOTS for n, s in enumerate(t_users)}
        o_users = [s for s in order if s[0] == "attend" and s[1] < MULTI]

        block = ctx.enter_context(nc.Block())

        @block.sync
        def _(sp):
            sp.dma_start(xs[0][:, :], x[0]).then_inc(x_in[0], 16)
            sp.dma_start(w[0][:, :], weights[0]).then_inc(w_in[0], 16)
            sp.dma_start(xs[1][:, :], x[1]).then_inc(x_in[1], 16)
            sp.dma_start(selections[:, :], row_selections).then_inc(selections_in, 16)
            for l in range(1, BLOCKS):
                sp.dma_start(w[l][:, :], weights[l]).then_inc(w_in[l], 16)
            for step in order:
                kind, l, b, i = step
                if kind == "write":
                    sp.wait_ge(x_ready, nth("residual", l, b, i))
                    half = slice(i * CHUNK, (i + 1) * CHUNK)
                    sp.dma_start(out[b][:, half], xs[b][:, half]).then_inc(out_written, 16)
            sp.wait_ge(out_written, 16 * B * NCH)

        @block.gpsimd
        def _(pool):
            for b in range(B):
                nc.gpsimd.memset(neg_max[b][:, :, :, :], 0.0).then_inc(max_zeros_ready, 1)
                nc.gpsimd.memset(v_heads[b][:, :, :, :], 1.0).then_inc(v_ones_ready, 1)
            nc.gpsimd.memset(q_heads[1][:, :, :].bitcast(F32), 0.0).then_inc(zeros_ready[1], 1)
            pool.wait_ge(const_in, 16)
            for kind, l, b, i in order:
                if kind == "rsqrt":
                    pool.wait_ge(variance_ready, nth("variance", l, b))
                    nc.gpsimd.tensor_tensor(grp[b][:, 1:2], grp[b][:, 0:1], minus_half,
                                            ALU.pow).then_inc(rsqrt_ready, 1)

        @block.tensor
        def _(pe):
            mm = nc.tensor.matmul

            def ring_free(step):
                n = w_users.index(step)
                if n < WORK:
                    return
                filler = w_users[n - WORK]
                reader = read_by(filler)
                if reader[0] == "row_max":
                    pe.wait_ge(max_done, nth(*reader))
                elif reader[0] == "exps":
                    pe.wait_ge(exps_done, nth(*reader))
                elif reader[0] == "add_bias":
                    pe.wait_ge(bias_ready, nth(*reader))
                elif reader[0] == "store_q":
                    pe.wait_ge(q_stored_even, nth(*reader))
                    pe.wait_ge(q_stored_odd, nth(*reader))
                elif reader[0] == "store_k":
                    pe.wait_ge(k_stored, nth(*reader))
                elif reader[0] == "split":
                    pe.wait_ge(qk_split, nth(*reader))
                elif reader[0] == "scale_q":
                    pe.wait_ge(q_scaled, nth(*reader))
                elif reader[0] == "round":
                    pe.wait_ge(qk_rounded, nth(*reader))
                elif reader[0] == "store_attended":
                    pe.wait_ge(att_stored, nth(*reader))
                elif reader[0] == "residual":
                    pe.wait_ge(x_ready, nth(*reader))

            for step in order:
                kind, l, b, i = step
                multi = l < MULTI
                m = ps_m[b]
                if kind == "warm":
                    if i == 0:
                        pe.wait_ge(warm_ready, 1)
                    used = [s for s in order[:order.index(step)] if s in o_users]
                    if used:
                        pe.wait_ge(out_stored, nth("store_out", *used[-1][1:]))
                    mm(ps_o[:, 0:C], blank[:, :], blank[:, :], start=True, stop=True)
                elif kind == "group_means":
                    if l == 0:
                        pe.wait_ge(const_in, 16)
                    else:
                        pe.wait_ge(x_ready, nth("residual", l - 1, b))
                    mm(m[:, 0:3], group_avg, const[:, EPS_COL + 3 * l:EPS_COL + 3 * (l + 1)], start=True, stop=False)
                    pe.wait_ge(moments_done, nth("moments", l, b))
                    mm(m[:, 0:3], group_avg, mom[b][:, 0:5:2], start=False, stop=True).then_inc(means_done, 1)
                elif kind == "fold_bias":
                    if l == 0:
                        pe.wait_ge(vec_in, 16)
                    pe.wait_ge(w_in[l], 16)
                    ring_free(step)
                    for n in range(3):
                        last = mm(ps_w[w_slot[step]][:, n:n + 1], w[l][:, n, :], vec[:, l, GN_B:GN_B + 1],
                                  start=True, stop=True)
                    last.then_inc(bias_folded, 1)
                elif kind == "project":
                    if i == 0:
                        pe.wait_ge(w_scaled, nth("scale_w", l, 0))
                        pe.wait_ge(h_ready, nth("normalise", l, b))
                    ring_free(step)
                    mm(ps_w[w_slot[step]][:, 0:T], ws[l][:, i, :], hn[b][:, :],
                       start=True, stop=True).then_inc(qk_projected, 1)
                elif kind == "project_v":
                    pe.wait_ge(w_scaled, nth("scale_w", l, 0))
                    pe.wait_ge(h_ready, nth("normalise", l, b))
                    for n in range(NCH):
                        last = mm(m[:, n * C:(n + 1) * C], hn[b][:, n * CHUNK:(n + 1) * CHUNK], ws[l][:, 2, :],
                                  start=True, stop=True)
                    last.then_inc(v_projected, 1)
                elif kind in ("place_q", "place_k"):
                    k = int(kind == "place_k")
                    pe.wait_ge(qk_split, nth("split", l, b, k))
                    if l == 0:
                        pe.wait_ge(select_ready, (i + 1) * PAIRS // STACKS)
                    ring_free(step)
                    for n in range(2):
                        dst = ps_w[w_slot[step]][:, n * T:(n + 1) * T]
                        pair = 2 * i + n
                        mm(dst, select[:, pair, 2 * k, :], qk_high[b][:, k, :], start=True, stop=False)
                        last = mm(dst, select[:, pair, 2 * k + 1, :], qk_low[b][:, k, :], start=False, stop=True)
                    last.then_inc(k_placed if k else q_placed, 1)
                elif kind == "scores" and multi:
                    if i % PER == 0:
                        pe.wait_ge(q_stored_even, nth("store_q", l, b, i // PER))
                        pe.wait_ge(q_stored_odd, nth("store_q", l, b, i // PER))
                        pe.wait_ge(k_stored, nth("store_k", l, b, i // PER))
                    ring_free(step)
                    for qc in range(NCH):
                        last = mm(ps_w[w_slot[step]][:, qc * T:(qc + 1) * T],
                                  q_heads[b][:, i, qc * CHUNK:(qc + 1) * CHUNK], k_pairs[b][:, i // 2, :],
                                  start=True, stop=True)
                    last.then_inc(scores_done, 1)
                elif kind == "scores":
                    pe.wait_ge(q_scaled, nth("scale_q", l, b, 0))
                    pe.wait_ge(qk_rounded, nth("round", l, b, 1))
                    ring_free(step)
                    mm(ps_w[w_slot[step]][:, 0:T], qk[b][:, 0, i * CHUNK:(i + 1) * CHUNK], qk[b][:, 1, :],
                       start=True, stop=True).then_inc(scores_done, 1)
                elif kind == "turn_max":
                    pe.wait_ge(max_done, nth("row_max", l, b, 2 * i + 1))
                    if i == 0:
                        pe.wait_ge(v_stored, nth("store_v", l, b))
                    else:
                        pe.wait_ge(max_stored, nth("store_max", l, b, i - 1))
                    for qc in range(NCH):
                        last = nc.tensor.transpose(m[0:QUAD + 1, qc * CHUNK:(qc + 1) * CHUNK], neg_max[b][:, i, qc, :],
                                                   ident)
                    last.then_inc(max_turned, 1)
                elif kind == "scores_t":
                    pair = i // 2
                    if i % 2 == 0:
                        pe.wait_ge(max_stored, nth("store_max", l, b, pair))
                    n = t_users.index(step)
                    if n >= SLOTS:
                        pe.wait_ge(exps_done, nth("exps", *t_users[n - SLOTS][1:]))
                    for kc in range(NCH):
                        dst = ps_t[t_slot[step]][:, kc * T:(kc + 1) * T]
                        keys = slice(kc * CHUNK, (kc + 1) * CHUNK)
                        last = mm(dst, k_pairs[b][:, pair, keys], q_heads[b][:, i, :], start=True, stop=True)
                    last.then_inc(scores_t_done, 1)
                elif kind == "attend" and multi:
                    pe.wait_ge(exps_done, nth("exps", l, b, PER * (i + 1) - 1))
                    if l == 0 and i == 0:
                        pe.wait_ge(v_ones_ready, b + 1)
                    pe.wait_ge(v_stored, nth("store_v", l, b))
                    n = o_users.index(step)
                    if n > 0:
                        pe.wait_ge(out_stored, nth("store_out", *o_users[n - 1][1:]))
                    for kc in range(NCH):
                        for j in range(PER):
                            h = PER * i + j
                            last = mm(ps_o[QUAD * j:QUAD * (j + 1), i * T:(i + 1) * T], v_heads[b][:, kc, h, :],
                                      probs[:, h, kc, :], start=(kc == 0), stop=(kc == NCH - 1))
                    last.then_inc(attended, 1)
                elif kind == "attend":
                    pe.wait_ge(p_stored, nth("store_p", l, b, i))
                    pe.wait_ge(v_stored, nth("store_v", l, b))
                    ring_free(step)
                    for kc in range(NCH):
                        last = mm(ps_w[w_slot[step]][:, 0:CHUNK], v_one[b][:, kc, :],
                                  pt_one[b][:, kc, i * CHUNK:(i + 1) * CHUNK], start=(kc == 0), stop=(kc == NCH - 1))
                    last.then_inc(attended, 1)
                elif kind == "turn_p":
                    pe.wait_ge(divided, nth("divide", l, b, i))
                    filler = t_users[t_users.index(step) - SLOTS]
                    if filler[0] == "scores_t":
                        pe.wait_ge(exps_done, nth(*read_by(filler)))
                    else:
                        pe.wait_ge(p_stored, nth(*read_by(filler)))
                    for kc in range(NCH):
                        last = nc.tensor.transpose(ps_t[t_slot[step]][:, kc * CHUNK:(kc + 1) * CHUNK],
                                                   p_one[b][:, i, kc * CHUNK:(kc + 1) * CHUNK], ident)
                    last.then_inc(p_turned, 1)
                elif kind == "turn_out":
                    pe.wait_ge(out_stored, nth("store_out", l, b, i))
                    if i == 0:
                        pe.wait_ge(max_stored, nth("store_max", l, b, PAIRS - 1))
                    else:
                        pe.wait_ge(divided, nth("divide", l, b, i - 1))
                    for qc in range(NCH):
                        at = (i * NCH + qc) * C
                        last = nc.tensor.transpose(m[:, at:at + C], o_raw[b][:, i, qc * CHUNK:(qc + 1) * CHUNK],
                                                   ident)
                    last.then_inc(out_turned, 1)
                elif kind == "turn_back":
                    pe.wait_ge(divided, nth("divide", l, b, STACKS - 1))
                    for qc in range(NCH):
                        last = nc.tensor.transpose(m[:, qc * CHUNK:(qc + 1) * CHUNK], o_tok[b][:, qc, :], ident)
                    last.then_inc(out_back, 1)
                elif kind == "project_out" and not multi:
                    pe.wait_ge(att_stored, nth("store_attended", l, b, i))
                    ring_free(step)
                    mm(ps_w[w_slot[step]][:, 0:CHUNK], w[l][:, 3, :], att[b][:, i * CHUNK:(i + 1) * CHUNK],
                       start=True, stop=True).then_inc(out_projected, 1)
                elif kind == "project_out":
                    pe.wait_ge(att_stored, nth("store_attended", l, b))
                    mm(m[:, 0:T], w[l][:, 3, :], att[b][:, :], start=True, stop=True).then_inc(out_projected, 1)

        @block.scalar
        def _(act):
            act.dma_start(const[:, :], constants).then_inc(const_in, 16)
            act.dma_start(vec[:, :, :], vectors).then_inc(vec_in, 16)
            act.wait_ge(warm_ready, 1)
            nc.scalar.activation(blank_exp[:, :], blank[:, 0:1], ACT.Exp)
            act.wait_ge(const_in, 16)
            act.wait_ge(vec_in, 16)
            for step in order:
                kind, l, b, i = step
                multi = l < MULTI
                m = ps_m[b]
                if kind == "select":
                    if i == 0:
                        act.wait_ge(selections_in, 16)
                    nc.scalar.activation(select[:, i, :, :].rearrange("p s c -> p (s c)"),
                                         selections[:, :], ACT.Copy,
                                         scale=const[:, PAIR_COL + i:PAIR_COL + i + 1]).then_inc(select_ready, 1)
                elif kind == "scale_w":
                    act.wait_ge(w_in[l], 16)
                    nc.scalar.activation(ws[l][:, :, :].rearrange("p n c -> p (n c)"),
                                         w[l][:, 0:3, :].rearrange("p n c -> p (n c)"), ACT.Copy,
                                         scale=vec[:, l, GN_W:GN_W + 1]).then_inc(w_scaled, 1)
                elif kind == "round":
                    act.wait_ge(bias_ready, nth("add_bias", l, 0))
                    act.wait_ge(qk_projected, nth("project", l, b, i))
                    dst = (qk_high if multi else qk)[b][:, i, :]
                    nc.scalar.activation(dst, ps_w[w_slot["project", l, b, i]][:, 0:T], ACT.Identity,
                                         bias=bias[:, l, i:i + 1]).then_inc(qk_rounded, 1)
                elif kind == "store_q":
                    act.wait_ge(q_placed, nth("place_q", l, b, i))
                    if l == 0:
                        act.wait_ge(zeros_ready[b], 1)
                    src = ps_w[w_slot["place_q", l, b, i]][0:HALF, :].rearrange("p (n t) -> p n t", n=2)
                    nc.scalar.activation(q_heads[b][0:HALF, PER * i:PER * (i + 1):2, :], src,
                                         ACT.Copy).then_inc(q_stored_even, 1)
                elif kind == "store_k":
                    act.wait_ge(k_placed, nth("place_k", l, b, i))
                    dst = k_pairs[b][:, 2 * i:2 * i + 2, :].rearrange("p n t -> p (n t)")
                    nc.scalar.activation(dst, ps_w[w_slot["place_k", l, b, i]][:, :], ACT.Identity,
                                         bias=ones_rows).then_inc(k_stored, 1)
                elif kind == "store_max":
                    act.wait_ge(max_turned, nth("turn_max", l, b, i))
                    for odd in range(2):
                        row = HALF * odd + MAX_ROW
                        last = nc.scalar.activation(q_heads[b][row:row + 1, 2 * i + odd, :],
                                                    m[QUAD * odd:QUAD * odd + 1, 0:T], ACT.Copy)
                    last.then_inc(max_stored, 1)
                elif kind == "exps" and multi:
                    act.wait_ge(scores_t_done, nth("scores_t", l, b, i))
                    if i % PER == 0:
                        users = [s for s in order[:order.index(step)] if s[0] == "attend" and s[3] == i // PER]
                        if users:
                            act.wait_ge(attended, nth(*users[-1]))
                    src = ps_t[t_slot["scores_t", l, b, i]][:, :]
                    nc.scalar.activation(probs[:, i, :, :].rearrange("p c t -> p (c t)"), src, ACT.Exp,
                                         scale=SCALE).then_inc(exps_done, 1)
                elif kind == "exps":
                    act.wait_ge(max_done, nth("row_max", l, b, i))
                    nc.scalar.activation(p_one[b][:, i, :], ps_w[w_slot["scores", l, b, i]][:, 0:T], ACT.Exp,
                                         bias=neg_max_one[b][:, i:i + 1],
                                         accum_out=sums[b][:, i:i + 1]).then_inc(exps_done, 1)
                elif kind == "store_p":
                    act.wait_ge(p_turned, nth("turn_p", l, b, i))
                    nc.scalar.activation(pt_one[b][:, :, i * CHUNK:(i + 1) * CHUNK],
                                         ps_t[t_slot["turn_p", l, b, i]][:, 0:T].rearrange("p (c q) -> p c q", c=NCH),
                                         ACT.Copy).then_inc(p_stored, 1)
                elif kind == "store_out":
                    act.wait_ge(attended, nth("attend", l, b, i))
                    nc.scalar.activation(o_raw[b][:, i, :], ps_o[:, i * T:(i + 1) * T],
                                         ACT.Copy).then_inc(out_stored, 1)

        @block.vector
        def _(dve):
            links = [0]

            def link(ins):
                links[0] += 1
                ins.then_inc(vchain, 1)
                dve.wait_ge(vchain, links[0])

            nc.vector.memset(blank[:, :], 0.0).then_inc(warm_ready, 1)
            nc.vector.memset(q_heads[0][:, :, :].bitcast(F32), 0.0).then_inc(zeros_ready[0], 1)
            tt, ts, stt = nc.vector.tensor_tensor, nc.vector.tensor_scalar, nc.vector.scalar_tensor_tensor
            for step in order:
                kind, l, b, i = step
                multi = l < MULTI
                m = ps_m[b]
                if kind == "moments":
                    if l == 0:
                        dve.wait_ge(x_in[b], 16)
                    else:
                        dve.wait_ge(x_ready, nth("residual", l - 1, b))
                    link(nc.vector.bn_stats(bn[b][:, :], xs[b][:, :]))
                    link(nc.vector.bn_aggr(mom[b][:, 0:2], bn[b][:, :]))
                    ts(mom[b][:, 2:3], mom[b][:, 0:1], -1.0, None, ALU.mult)
                    stt(out=mom[b][:, 4:5], in0=mom[b][:, 0:1], scalar=mom[b][:, 0:1], in1=mom[b][:, 1:2],
                        op0=ALU.mult, op1=ALU.add).then_inc(moments_done, 1)
                elif kind == "variance":
                    dve.wait_ge(means_done, nth("group_means", l, b))
                    ts(grp[b][:, 0:1], m[:, 0:1], m[:, 1:2], m[:, 2:3], ALU.mult, ALU.add).then_inc(variance_ready, 1)
                elif kind == "normalise":
                    dve.wait_ge(rsqrt_ready, nth("rsqrt", l, b))
                    ts(hn[b][:, :], xs[b][:, :], m[:, 0:1], grp[b][:, 1:2], ALU.subtract,
                       ALU.mult).then_inc(h_ready, 1)
                elif kind == "add_bias":
                    dve.wait_ge(bias_folded, nth("fold_bias", l, b))
                    tt(bias[:, l, :], ps_w[w_slot["fold_bias", l, b, 0]][:, 0:3], vec[:, l, BQ:BV + 1],
                       ALU.add).then_inc(bias_ready, 1)
                elif kind == "split":
                    dve.wait_ge(qk_rounded, nth("round", l, b, i))
                    stt(out=qk_low[b][:, i, :], in0=ps_w[w_slot["project", l, b, i]][:, 0:T],
                        scalar=bias[:, l, i:i + 1], in1=qk_high[b][:, i, :].bitcast(F32),
                        op0=ALU.add, op1=ALU.subtract).then_inc(qk_split, 1)
                elif kind == "store_v":
                    dve.wait_ge(v_projected, nth("project_v", l, b))
                    if multi:
                        if l == 0:
                            dve.wait_ge(v_ones_ready, b + 1)
                        dst = v_heads[b][:, :, :, 0:DH].rearrange("p c h d -> p (c h) d")
                        src = m[:, 0:NCH * C].rearrange("p (c d) -> p c d", d=DH)
                    else:
                        dst = v_one[b][:, :, :].rearrange("p c d -> p (c d)")
                        src = m[:, 0:NCH * C]
                    nc.vector.tensor_copy(dst, src).then_inc(v_stored, 1)
                elif kind == "store_attended":
                    if multi:
                        dve.wait_ge(out_back, nth("turn_back", l, b))
                        dst, src = att[b][:, :], m[:, 0:T]
                    else:
                        dve.wait_ge(attended, nth("attend", l, b, i))
                        dst = att[b][:, i * CHUNK:(i + 1) * CHUNK]
                        src = ps_w[w_slot["attend", l, b, i]][:, 0:CHUNK]
                    ts(dst, src, bias[:, l, 2:3], None, ALU.add).then_inc(att_stored, 1)
                elif kind == "store_q":
                    dve.wait_ge(q_placed, nth("place_q", l, b, i))
                    if l == 0:
                        dve.wait_ge(zeros_ready[b], 1)
                    src = ps_w[w_slot["place_q", l, b, i]][HALF:C, :].rearrange("p (n t) -> p n t", n=2)
                    nc.vector.tensor_copy(q_heads[b][HALF:C, PER * i + 1:PER * (i + 1):2, :],
                                          src).then_inc(q_stored_odd, 1)
                elif kind == "row_max" and multi:
                    dve.wait_ge(scores_done, nth("scores", l, b, i))
                    if l == 0:
                        dve.wait_ge(max_zeros_ready, b + 1)
                    nc.vector.tensor_reduce(neg_max[b][:, i // 2, :, QUAD * (i % 2)],
                                            ps_w[w_slot["scores", l, b, i]][:, :].rearrange("p (c t) -> p c t", c=NCH),
                                            AX_X, ALU.max, negate=True).then_inc(max_done, 1)
                elif kind == "row_max":
                    dve.wait_ge(scores_done, nth("scores", l, b, i))
                    nc.vector.tensor_reduce(neg_max_one[b][:, i:i + 1], ps_w[w_slot["scores", l, b, i]][:, 0:T],
                                            AX_X, ALU.max, negate=True).then_inc(max_done, 1)
                elif kind == "scale_q":
                    dve.wait_ge(qk_projected, nth("project", l, b, 0))
                    ts(qk[b][:, 0, :], ps_w[w_slot["project", l, b, 0]][:, 0:T], bias[:, l, 0:1], SCALE_ONE,
                       ALU.add, ALU.mult).then_inc(q_scaled, 1)
                elif kind == "divide" and multi:
                    dve.wait_ge(out_turned, nth("turn_out", l, b, i))
                    src = m[:, i * NCH * C:(i + 1) * NCH * C].rearrange("p (n e) -> p n e", e=2 * DH)
                    link(nc.vector.reciprocal(rden[b][:, i, :], src[:, :, DH:DH + 1].rearrange("p n e -> p (n e)")))
                    src = m[:, i * NCH * C:(i + 1) * NCH * C].rearrange("p (c j e) -> p c j e", c=NCH, e=2 * DH)
                    dst = o_tok[b][:, :, i * HALF:(i + 1) * HALF].rearrange("p c (j d) -> p c j d", d=DH)
                    by = rden[b][:, i, :].rearrange("p (c j) -> p c j", c=NCH).unsqueeze(3)
                    tt(dst, src[:, :, :, 0:DH], by.to_broadcast([C, NCH, PER, DH]), ALU.mult).then_inc(divided, 1)
                elif kind == "divide":
                    dve.wait_ge(exps_done, nth("exps", l, b, i))
                    link(nc.vector.reciprocal(rden[b][:, 0, i:i + 1], sums[b][:, i:i + 1]))
                    ts(p_one[b][:, i, :], p_one[b][:, i, :], rden[b][:, 0, i:i + 1], None,
                       ALU.mult).then_inc(divided, 1)
                elif kind == "residual":
                    dve.wait_ge(out_projected, nth("project_out", l, b, i))
                    if multi:
                        tokens, src = slice(0, T), m[:, 0:T]
                    else:
                        tokens = slice(i * CHUNK, (i + 1) * CHUNK)
                        src = ps_w[w_slot["project_out", l, b, i]][:, 0:CHUNK]
                    stt(out=xs[b][:, tokens], in0=src, scalar=vec[:, l, BP:BP + 1], in1=xs[b][:, tokens],
                        op0=ALU.add, op1=ALU.add).then_inc(x_ready, 1)


def kernel(**inputs):
    import numpy as np
    import concourse.bacc as bacc
    from concourse.bass_utils import run_bass_kernel_spmd

    a = {k: np.asarray(v) for k, v in inputs.items()}
    wq, wk, wv, wp = {}, {}, {}, {}
    bq, bk, bv, bp, gw, gb = {}, {}, {}, {}, {}, {}
    p = "L0_conv_"
    wq[0], wk[0], wv[0], wp[0] = (a[p + n] for n in ("wq", "wk", "wv", "wp"))
    bq[0], bk[0], bv[0], bp[0] = (a[p + n] for n in ("bq", "bk", "bv", "bp"))
    gw[0], gb[0] = a[p + "gn_w"], a[p + "gn_b"]
    p = "L1_conv_"
    wq[1], wk[1], wv[1] = (a[p + "w1"][n * C:(n + 1) * C] for n in range(3))
    bq[1], bk[1], bv[1] = (a[p + "b1"][n * C:(n + 1) * C] for n in range(3))
    wp[1], bp[1], gw[1], gb[1] = a[p + "w2"], a[p + "b2"], a[p + "gn_w"], a[p + "gn_b"]
    p = "L2_conv_"
    wq[2], bq[2], wp[2], bp[2] = a[p + "wq"], a[p + "bq"], a[p + "wproj"], a[p + "bproj"]
    wk[2], wv[2] = (a[p + "wkv"][n * C:(n + 1) * C] for n in range(2))
    bk[2], bv[2] = (a[p + "bkv"][n * C:(n + 1) * C] for n in range(2))
    gw[2], gb[2] = a[p + "gn_weight"], a[p + "gn_bias"]
    p = "L3_conv_"
    wq[3], wk[3], wv[3] = (a[p + "qkv_w"][n * C:(n + 1) * C] for n in range(3))
    bq[3], bk[3], bv[3] = (a[p + "qkv_b"][n * C:(n + 1) * C] for n in range(3))
    wp[3], bp[3], gw[3], gb[3] = a[p + "proj_w"], a[p + "proj_b"], a[p + "gn_scale"], a[p + "gn_bias"]

    vectors = np.zeros((C, BLOCKS, NVEC), np.float32)
    arrays = {"x": np.ascontiguousarray(a["x"].reshape(B, C, T))}
    for l in range(BLOCKS):
        arrays[f"w{l}"] = np.ascontiguousarray(np.stack([wq[l].T, wk[l].T, wv[l].T, wp[l].T], axis=1))
        for at, v in ((GN_W, gw), (GN_B, gb), (BQ, bq), (BK, bk), (BV, bv), (BP, bp)):
            vectors[:, l, at] = v[l]
    arrays["vectors"] = vectors
    constants = np.zeros((C, NCONST), np.float32)
    selections = np.zeros((C, SELS * C), np.float32)
    constants[:, 0:C] = np.eye(C)
    constants[:, C:2 * C] = np.kron(np.eye(C // GROUP), np.full((GROUP, GROUP), 1.0 / GROUP))
    one, none, gap = np.eye(DH), np.zeros((DH, DH)), np.zeros((DH, HALF - 3 * DH - 1))
    for n, (first, second, third) in enumerate(((one, none, one), (none, one, none),
                                                (one, one, none), (none, none, one))):
        of_head = np.concatenate([first, second, np.zeros((DH, 1)), third, gap], axis=1)
        of_pair = np.kron(np.eye(2), of_head)
        selections[:, n * C:(n + 1) * C] = np.tile(of_pair, (PAIRS, 1))
    constants[:, PAIR_COL:PAIR_COL + PAIRS] = np.kron(np.eye(PAIRS), np.ones((C // PAIRS, 1)))
    constants[[MAX_ROW, HALF + MAX_ROW], ONES_COL] = 1.0
    constants[:, HALF_COL] = -0.5
    constants[:, EPS_COL:NCONST] = np.kron(EPS, [0.0, 0.0, 1.0])
    arrays["constants"], arrays["selections"] = constants, selections

    nc = bacc.Bacc("TRN2", target_bir_lowering=False, num_devices=1)
    ap = {n: nc.dram_tensor(f"in_{n}", v.shape, mybir.dt.float32, kind="ExternalInput").ap() for n, v in arrays.items()}
    out = nc.dram_tensor("out", (B, C, T), mybir.dt.float32, kind="ExternalOutput").ap()
    attention_blocks(nc, ap["x"], out, ap["vectors"], ap["constants"], ap["selections"],
                     [ap[f"w{l}"] for l in range(BLOCKS)])
    r = run_bass_kernel_spmd(nc, [{f"in_{n}": v for n, v in arrays.items()}], core_ids=[0])
    return r.results[0]["out"].reshape(a["x"].shape)
```
